# Optimizing a Trainium2 kernel written in Bass

```python
import numpy as np
import jax
import jax.numpy as jnp

def _softmax(x, axis=-1):
    return jax.nn.softmax(x, axis=axis)

def _gelu(x):
    return jax.nn.gelu(x, approximate=True)

def _silu(x):
    return jax.nn.silu(x)

def _sigmoid(x):
    return jax.nn.sigmoid(x)

def _layernorm(x, axis=-1, eps=1e-05):
    m = jnp.mean(x, axis=axis, keepdims=True)
    v = jnp.var(x, axis=axis, keepdims=True)
    return (x - m) / jnp.sqrt(v + eps)

def _scatter_add(tgt, idx, src, axis=0):
    return tgt.at[idx].add(src)

def _segment_sum(src, seg, n):
    return jax.ops.segment_sum(src, seg, n)
kernel_name = 'mk_dlrm_tower_d1_rec_r8_6264ca'

def setup_inputs(seed: int=0):
    np.random.seed(seed)
    _w = jnp.asarray

    def _rec_inputs():
        import jax
        import jax.numpy as jnp
        _tk = jax.random.key(seed)
        dense_ctx = jax.random.normal(jax.random.fold_in(_tk, 190), (2048, 16), jnp.float32)
        ids = jnp.stack([jax.random.randint(jax.random.fold_in(_tk, 200 + f), (2048,), 0, v, jnp.int32) for f, v in enumerate([12500, 1250, 1250, 12500, 12500, 1250, 1250, 1000, 1000, 12500, 125000, 1250, 12500, 12500, 12500, 12500, 1000, 1000, 1000, 1000, 1250, 1000, 1000, 1250, 1000, 1250, 1000])], axis=1)
        tbl_0 = 0.05 * jax.random.normal(jax.random.fold_in(_tk, 500 + 0), (12500, 128), jnp.float32)
        tbl_1 = 0.05 * jax.random.normal(jax.random.fold_in(_tk, 500 + 1), (1250, 128), jnp.float32)
        tbl_2 = 0.05 * jax.random.normal(jax.random.fold_in(_tk, 500 + 2), (1250, 128), jnp.float32)
        tbl_3 = 0.05 * jax.random.normal(jax.random.fold_in(_tk, 500 + 3), (12500, 128), jnp.float32)
        tbl_4 = 0.05 * jax.random.normal(jax.random.fold_in(_tk, 500 + 4), (12500, 128), jnp.float32)
        tbl_5 = 0.05 * jax.random.normal(jax.random.fold_in(_tk, 500 + 5), (1250, 128), jnp.float32)
        tbl_6 = 0.05 * jax.random.normal(jax.random.fold_in(_tk, 500 + 6), (1250, 128), jnp.float32)
        tbl_7 = 0.05 * jax.random.normal(jax.random.fold_in(_tk, 500 + 7), (1000, 128), jnp.float32)
        tbl_8 = 0.05 * jax.random.normal(jax.random.fold_in(_tk, 500 + 8), (1000, 128), jnp.float32)
        tbl_9 = 0.05 * jax.random.normal(jax.random.fold_in(_tk, 500 + 9), (12500, 128), jnp.float32)
        tbl_10 = 0.05 * jax.random.normal(jax.random.fold_in(_tk, 500 + 10), (125000, 128), jnp.float32)
        tbl_11 = 0.05 * jax.random.normal(jax.random.fold_in(_tk, 500 + 11), (1250, 128), jnp.float32)
        tbl_12 = 0.05 * jax.random.normal(jax.random.fold_in(_tk, 500 + 12), (12500, 128), jnp.float32)
        tbl_13 = 0.05 * jax.random.normal(jax.random.fold_in(_tk, 500 + 13), (12500, 128), jnp.float32)
        tbl_14 = 0.05 * jax.random.normal(jax.random.fold_in(_tk, 500 + 14), (12500, 128), jnp.float32)
        tbl_15 = 0.05 * jax.random.normal(jax.random.fold_in(_tk, 500 + 15), (12500, 128), jnp.float32)
        tbl_16 = 0.05 * jax.random.normal(jax.random.fold_in(_tk, 500 + 16), (1000, 128), jnp.float32)
        tbl_17 = 0.05 * jax.random.normal(jax.random.fold_in(_tk, 500 + 17), (1000, 128), jnp.float32)
        tbl_18 = 0.05 * jax.random.normal(jax.random.fold_in(_tk, 500 + 18), (1000, 128), jnp.float32)
        tbl_19 = 0.05 * jax.random.normal(jax.random.fold_in(_tk, 500 + 19), (1000, 128), jnp.float32)
        tbl_20 = 0.05 * jax.random.normal(jax.random.fold_in(_tk, 500 + 20), (1250, 128), jnp.float32)
        tbl_21 = 0.05 * jax.random.normal(jax.random.fold_in(_tk, 500 + 21), (1000, 128), jnp.float32)
        tbl_22 = 0.05 * jax.random.normal(jax.random.fold_in(_tk, 500 + 22), (1000, 128), jnp.float32)
        tbl_23 = 0.05 * jax.random.normal(jax.random.fold_in(_tk, 500 + 23), (1250, 128), jnp.float32)
        tbl_24 = 0.05 * jax.random.normal(jax.random.fold_in(_tk, 500 + 24), (1000, 128), jnp.float32)
        tbl_25 = 0.05 * jax.random.normal(jax.random.fold_in(_tk, 500 + 25), (1250, 128), jnp.float32)
        tbl_26 = 0.05 * jax.random.normal(jax.random.fold_in(_tk, 500 + 26), (1000, 128), jnp.float32)
        _rk = jax.random.fold_in(_tk, 7)
        W_top1 = 0.0521996 * jax.random.normal(jax.random.fold_in(_tk, 801), (367, 512), jnp.float32)
        W_top2 = 0.0441942 * jax.random.normal(jax.random.fold_in(_tk, 802), (512, 256), jnp.float32)
        W_top3 = 0.0625 * jax.random.normal(jax.random.fold_in(_tk, 803), (256, 1), jnp.float32)
        b_top1 = jnp.zeros((512,), jnp.float32)
        b_top2 = jnp.zeros((256,), jnp.float32)
        return (dense_ctx, ids, tbl_0, tbl_1, tbl_2, tbl_3, tbl_4, tbl_5, tbl_6, tbl_7, tbl_8, tbl_9, tbl_10, tbl_11, tbl_12, tbl_13, tbl_14, tbl_15, tbl_16, tbl_17, tbl_18, tbl_19, tbl_20, tbl_21, tbl_22, tbl_23, tbl_24, tbl_25, tbl_26, W_top1, b_top1, W_top2, b_top2, W_top3)
    dense_ctx, ids, tbl_0, tbl_1, tbl_2, tbl_3, tbl_4, tbl_5, tbl_6, tbl_7, tbl_8, tbl_9, tbl_10, tbl_11, tbl_12, tbl_13, tbl_14, tbl_15, tbl_16, tbl_17, tbl_18, tbl_19, tbl_20, tbl_21, tbl_22, tbl_23, tbl_24, tbl_25, tbl_26, W_top1, b_top1, W_top2, b_top2, W_top3 = _rec_inputs()

    def _L0_rec_setup():
        import jax, jax.numpy as jnp
        import numpy as np
        B, F, D = (2048, 27, 128)
        _TRIL_I, _TRIL_J = np.tril_indices(F, k=-1)
        key = jax.random.key(seed)
        features = jax.random.normal(key, (B, F, D), dtype=jnp.float32)
        return {'features': features}
    _L0_rec_all = _L0_rec_setup()
    _L0_rec_in = {k: v for k, v in _L0_rec_all.items() if k in ()}
    del _L0_rec_all
    return {'dense_ctx': dense_ctx, 'ids': ids, 'tbl_0': tbl_0, 'tbl_1': tbl_1, 'tbl_2': tbl_2, 'tbl_3': tbl_3, 'tbl_4': tbl_4, 'tbl_5': tbl_5, 'tbl_6': tbl_6, 'tbl_7': tbl_7, 'tbl_8': tbl_8, 'tbl_9': tbl_9, 'tbl_10': tbl_10, 'tbl_11': tbl_11, 'tbl_12': tbl_12, 'tbl_13': tbl_13, 'tbl_14': tbl_14, 'tbl_15': tbl_15, 'tbl_16': tbl_16, 'tbl_17': tbl_17, 'tbl_18': tbl_18, 'tbl_19': tbl_19, 'tbl_20': tbl_20, 'tbl_21': tbl_21, 'tbl_22': tbl_22, 'tbl_23': tbl_23, 'tbl_24': tbl_24, 'tbl_25': tbl_25, 'tbl_26': tbl_26, 'W_top1': W_top1, 'b_top1': b_top1, 'W_top2': W_top2, 'b_top2': b_top2, 'W_top3': W_top3}

def reference(dense_ctx, ids, tbl_0, tbl_1, tbl_2, tbl_3, tbl_4, tbl_5, tbl_6, tbl_7, tbl_8, tbl_9, tbl_10, tbl_11, tbl_12, tbl_13, tbl_14, tbl_15, tbl_16, tbl_17, tbl_18, tbl_19, tbl_20, tbl_21, tbl_22, tbl_23, tbl_24, tbl_25, tbl_26, W_top1, b_top1, W_top2, b_top2, W_top3):
    import jax
    import jax.numpy as jnp

    def _L0_rec_ref(features):
        import jax, jax.numpy as jnp
        import numpy as np
        B, F, D = (2048, 27, 128)
        _TRIL_I, _TRIL_J = np.tril_indices(F, k=-1)
        xactions = jnp.einsum('bfd,bgd->bfg', features, features)
        activations = xactions[:, _TRIL_I, _TRIL_J]
        return activations
    e = jnp.stack([tbl_0[ids[:, 0]], tbl_1[ids[:, 1]], tbl_2[ids[:, 2]], tbl_3[ids[:, 3]], tbl_4[ids[:, 4]], tbl_5[ids[:, 5]], tbl_6[ids[:, 6]], tbl_7[ids[:, 7]], tbl_8[ids[:, 8]], tbl_9[ids[:, 9]], tbl_10[ids[:, 10]], tbl_11[ids[:, 11]], tbl_12[ids[:, 12]], tbl_13[ids[:, 13]], tbl_14[ids[:, 14]], tbl_15[ids[:, 15]], tbl_16[ids[:, 16]], tbl_17[ids[:, 17]], tbl_18[ids[:, 18]], tbl_19[ids[:, 19]], tbl_20[ids[:, 20]], tbl_21[ids[:, 21]], tbl_22[ids[:, 22]], tbl_23[ids[:, 23]], tbl_24[ids[:, 24]], tbl_25[ids[:, 25]], tbl_26[ids[:, 26]]], axis=1)
    z = _L0_rec_ref(e)
    z = z.reshape(z.shape[0], -1)
    h = jnp.concatenate([z, dense_ctx], axis=1)
    h = jnp.maximum(h @ W_top1 + b_top1, 0.0)
    h = jnp.maximum(h @ W_top2 + b_top2, 0.0)
    y = h @ W_top3
    return y

_drawn_inputs = setup_inputs


def setup_inputs(seed=0):
    import zlib

    import numpy as np

    out = dict(_drawn_inputs(seed))
    spreads = {'b_top1': (0.0, 0.1), 'b_top2': (0.0, 0.1)}
    factors = {}
    for name, (base, spread) in spreads.items():
        noise = np.random.default_rng([zlib.crc32(name.encode()), seed]).standard_normal(out[name].shape)
        drawn = base * np.exp(spread * noise) if base else spread * noise
        out[name] = jnp.asarray(drawn.astype(out[name].dtype))
    for name, factor in factors.items():
        out[name] = (out[name] * factor).astype(out[name].dtype)
    return out
```

```python
import concourse.bass as bass
from concourse import mybir
from contextlib import ExitStack

VOCAB = [12500, 1250, 1250, 12500, 12500, 1250, 1250, 1000, 1000, 12500, 125000, 1250, 12500, 12500,
         12500, 12500, 1000, 1000, 1000, 1000, 1250, 1000, 1000, 1250, 1000, 1250, 1000]
F = len(VOCAB)
D = 128
SAMPLES = 2048
DENSE = 16
H1, H2 = 512, 256

P = 128
BLOCK = 256
BLOCKS = SAMPLES // BLOCK
HALVES = BLOCK // P
CHUNKS = 8
PICKED = [f for f in range(F) if VOCAB[f] == 1000][:7]
GATHERED = [f for f in range(F) if f not in PICKED]
ROWS = 1000 // CHUNKS
PLACES = GATHERED + PICKED
NG, NP = len(GATHERED), len(PICKED)
PARTS = 3
GROUP = 4
GROUPS = NG // GROUP
TBANKS = HALVES * GROUPS
PBANKS = (NP + 1) // 2
QUADS = 4
SPAN = BLOCK // QUADS
HSPAN = P // QUADS
FILL = 16
GBANKS = BLOCK // (QUADS * FILL)
RING = (F - 1) // 2
WRAPPED = F + RING
ZCHUNKS = 3
AROWS = F // ZCHUNKS
ZROWS = AROWS * RING
DROWS = [0, 5, 11]
DFROM = [0, 0, 5]
N1, N2 = H1 // P, H2 // P


def pair_rows():
    rows = []
    for a in range(F):
        for k in range(1, RING + 1):
            i, j = PLACES[a], PLACES[(a + k) % F]
            i, j = max(i, j), min(i, j)
            rows.append(i * (i - 1) // 2 + j)
    return rows


def dlrm_tower(nc, ids_g, ids_p, tables, dense_t, w1_pairs, w1_dense, b1, w2, b2, w3, out):
    f32, bf16, i32, f16 = mybir.dt.float32, mybir.dt.bfloat16, mybir.dt.int32, mybir.dt.float16
    ALU = mybir.AluOpType
    ACT = mybir.ActivationFunctionType

    ctx = ExitStack()
    with ctx:
        def sb(name, shape, dt):
            return ctx.enter_context(nc.sbuf_tensor(name, shape, dt))

        def pb(name):
            return ctx.enter_context(nc.psum_tensor(name, [P, 512], f32))

        def sem(name):
            return ctx.enter_context(nc.semaphore(name))

        idx = sb("idx", [P, 2, HALVES, NG], i32)
        emb = sb("emb", [P, 2, HALVES, NG, D], f32)
        emb_t = sb("emb_t", [P, 2, F, BLOCK], f32)
        parts = sb("parts", [ROWS, NP, PARTS, CHUNKS, D], bf16)
        stage = sb("stage", [ROWS, 2, CHUNKS * D], f32)
        rest = sb("rest", [ROWS, CHUNKS * D], f32)
        ids_wide = sb("ids_wide", [ROWS, NP, BLOCK], i32)
        ids_half = sb("ids_half", [ROWS, NP, BLOCK], f16)
        row_int = sb("row_int", [P, CHUNKS], i32)
        row_no = sb("row_no", [P, CHUNKS], f32)
        onehot = sb("onehot", [ROWS, 4, 2, 2 * BLOCK], bf16)
        ident = sb("ident", [P, P], f32)
        gram = sb("gram", [P, F, SPAN], f32)
        z = sb("z", [P, 2, ZCHUNKS, BLOCK], f32)
        w1_sb = sb("w1_sb", [P, ZCHUNKS, H1], f32)
        w2_sb = sb("w2_sb", [P, N1, H2], f32)
        w3_sb = sb("w3_sb", [P, N2], f32)
        b1_sb = sb("b1_sb", [P, N1], f32)
        b2_sb = sb("b2_sb", [P, N2], f32)
        hid1 = sb("hid1", [P, N1, BLOCK], f32)
        hid2 = sb("hid2", [P, N2, BLOCK], f32)
        y_sb = sb("y_sb", [P, BLOCKS, HALVES], f32)

        gram_dram = nc.dram_tensor("gram_dram", (2, QUADS, 32, WRAPPED, SPAN), f32, kind="Internal").ap()

        p_turn = [pb(f"p_turn{i}") for i in range(2)]
        p_pick = [pb(f"p_pick{i}") for i in range(2)]
        p_gram = [pb(f"p_gram{i}") for i in range(2)]
        p_mlp = [pb(f"p_mlp{i}") for i in range(2)]

        table_in = [sem(f"table_in{i}") for i in range(2)]
        weights_in = sem("weights_in")
        idx_in = [sem(f"idx_in{i}") for i in range(2)]
        wide_in = sem("wide_in")
        gathers_begun = sem("gathers_begun")
        gathered = [[[sem(f"gathered{p}{h}{g}") for g in range(GROUPS)] for h in range(HALVES)]
                    for p in range(2)]
        ident_zeroed = sem("ident_zeroed")
        ident_made = sem("ident_made")
        rows_counted = sem("rows_counted")
        rows_known = sem("rows_known")
        gram_zeroed = sem("gram_zeroed")
        part_high = sem("part_high")
        part_rest = sem("part_rest")
        part_mid = sem("part_mid")
        table_split = sem("table_split")
        ids_halved = sem("ids_halved")
        onehot_made = sem("onehot_made")
        onehot_used = sem("onehot_used")
        picked_copied = sem("picked_copied")
        turned = sem("turned")
        turned_copied = sem("turned_copied")
        gram_done = sem("gram_done")
        gram_copied = sem("gram_copied")
        gram_stored = sem("gram_stored")
        z_in = [sem(f"z_in{i}") for i in range(2)]
        sum1_done = sem("sum1_done")
        hid1_ready = sem("hid1_ready")
        sum2_done = sem("sum2_done")
        hid2_ready = sem("hid2_ready")
        y_done = sem("y_done")
        y_copied = sem("y_copied")
        y_stored = sem("y_stored")

        WEIGHT_LOADS = ZCHUNKS + 2 + 4
        Z_LOADS = ZCHUNKS * QUADS + 2

        def blocks(eng, step):
            step(0, 0, 0)
            with eng.Fori(0, BLOCKS // 2 - 1) as i:
                step(i * 2 + 1, 1, i)
                step(i * 2 + 2, 0, i + 1)
            step(BLOCKS - 1, 1, BLOCKS // 2 - 1)

        block = ctx.enter_context(nc.Block())

        @block.sync
        def _(sp):
            def load_idx(b, p):
                sp.dma_start(idx[:, p], ids_g[bass.ds(b, 1)].rearrange("o p h g -> (o p) h g"))\
                    .then_inc(idx_in[p], 16)

            def load_wide(b):
                sp.dma_start(ids_wide[:], ids_p[bass.ds(b, 1)].rearrange("o n s -> o (n s)")
                             .broadcast_to([ROWS, NP * BLOCK]))\
                    .then_inc(wide_in, 16)

            load_idx(0, 0)
            load_wide(0)
            for n in range(NP):
                if n >= 2:
                    sp.wait_ge(part_high, n - 1)
                    sp.wait_ge(part_rest, n - 1)
                sp.dma_start(stage[:, n % 2], tables[PICKED[n]].rearrange("(p c) d -> p (c d)", c=CHUNKS))\
                    .then_inc(table_in[n % 2], 16)
            for c in range(ZCHUNKS):
                sp.dma_start(w1_sb[0:ZROWS, c], w1_pairs[c * ZROWS:(c + 1) * ZROWS, :]).then_inc(weights_in, 16)
                if DROWS[c]:
                    sp.dma_start(w1_sb[ZROWS:ZROWS + DROWS[c], c], w1_dense[DFROM[c]:DFROM[c] + DROWS[c], :])\
                        .then_inc(weights_in, 16)
            sp.dma_start(w2_sb[:], w2.rearrange("(k p) n -> p k n", p=P)).then_inc(weights_in, 16)
            with nc.allow_non_contiguous_dma(reason="small vectors, one value per partition"):
                sp.dma_start(w3_sb[:], w3.rearrange("(k p) o -> p (k o)", p=P)).then_inc(weights_in, 16)
                sp.dma_start(b1_sb[:], b1.rearrange("(k p) -> p k", p=P)).then_inc(weights_in, 16)
                sp.dma_start(b2_sb[:], b2.rearrange("(k p) -> p k", p=P)).then_inc(weights_in, 16)

            def step(b, p, u):
                last = isinstance(b, int) and b == BLOCKS - 1
                if not last:
                    if not isinstance(b, int):
                        sp.wait_ge(turned, b * TBANKS)
                    load_idx(b + 1, 1 - p)
                    sp.wait_ge(ids_halved, b + 1)
                    load_wide(b + 1)
                sp.wait_ge(gram_copied, (b + 1) * GBANKS)
                rows = gram_dram[p].rearrange("q a b s -> (q a) b s")
                sp.dma_start(rows[:, 0:F], gram[:]).then_inc(gram_stored, 16)
                sp.dma_start(rows[:, F:WRAPPED], gram[:, 0:RING]).then_inc(gram_stored, 16)
                sp.wait_ge(gram_stored, (b + 1) * 32)
                for c in range(ZCHUNKS):
                    for q in range(QUADS):
                        pairs = bass.AP(gram_dram.tensor,
                                        ((p * QUADS + q) * 32 + c * AROWS) * WRAPPED * SPAN
                                        + (c * AROWS + 1) * SPAN,
                                        [[(WRAPPED + 1) * SPAN, AROWS], [SPAN, RING], [1, SPAN]])
                        sp.dma_start(z[0:ZROWS, p, c, q * SPAN:(q + 1) * SPAN], pairs).then_inc(z_in[p], 16)
                    if DROWS[c]:
                        sp.dma_start(z[ZROWS:ZROWS + DROWS[c], p, c],
                                     dense_t[DFROM[c]:DFROM[c] + DROWS[c], bass.ds(b, 1), :]
                                     .rearrange("d o s -> d (o s)")).then_inc(z_in[p], 16)

            blocks(sp, step)
            sp.wait_ge(y_copied, BLOCKS + 1)
            sp.dma_start(out, y_sb[:].rearrange("p b h -> p (b h)")).then_inc(y_stored, 16)
            sp.wait_ge(y_stored, 16)

        @block.gpsimd
        def _(pool):
            pool.iota(row_int[:], pattern=[[1, CHUNKS]], base=0, channel_multiplier=CHUNKS)\
                .then_inc(rows_counted, 1)
            pool.memset(ident[:], 0.0).then_inc(ident_zeroed, 1)
            pool.wait_ge(ident_zeroed, 1)
            pool.affine_select(out=ident[:], in_=ident[:], compare_op=ALU.not_equal, fill=1.0, base=0,
                               pattern=[[-1, P]], channel_multiplier=1).then_inc(ident_made, 1)

            def step(b, p, u):
                pool.wait_ge(idx_in[p], (u + 1) * 16)
                pool.sem_inc(gathers_begun, 1)
                for h in range(HALVES):
                    for g in range(NG):
                        pool.indirect_dma_start(
                            emb[:, p, h, g], None, tables[GATHERED[g]],
                            bass.IndirectOffsetOnAxis(idx[:, p, h, g:g + 1], 0),
                        ).then_inc(gathered[p][h][g // GROUP], 16)

            blocks(pool, step)

        @block.tensor
        def _(pe):
            def turn(b, p, u):
                for h in range(HALVES):
                    for g in range(GROUPS):
                        r = h * GROUPS + g
                        pe.wait_ge(gathered[p][h][g], (u + 1) * (16 * GROUP))
                        if not (isinstance(b, int) and b == 0 and r < 2):
                            pe.wait_ge(turned_copied, b * TBANKS + (r - 1))
                        for k in range(GROUP):
                            last = pe.transpose(p_turn[r % 2][:, k * P:(k + 1) * P],
                                                emb[:, p, h, g * GROUP + k], ident[:])
                        last.then_inc(turned, 1)

            def grams(b, p):
                pe.wait_ge(turned_copied, (b + 1) * TBANKS)
                pe.wait_ge(picked_copied, (b + 1) * PBANKS)
                for v in range(GBANKS):
                    h, from_ = v // (HSPAN // FILL), v % (HSPAN // FILL) * FILL
                    if not (isinstance(b, int) and b == 0 and v < 2):
                        pe.wait_ge(gram_copied, b * GBANKS + (v - 1))
                    for k in range(FILL):
                        for q in range(QUADS):
                            s = h * P + q * HSPAN + from_ + k
                            e = emb_t[:, p, :, s]
                            last = pe.matmul(p_gram[v % 2][32 * q:32 * q + F, k * F:(k + 1) * F],
                                             e, e, start=True, stop=True)
                    last.then_inc(gram_done, 1)

            def pick(b, w, ints):
                pair = range(2 * w, min(2 * w + 2, NP))
                if ints:
                    pe.wait_ge(table_split, pair[-1] + 1)
                if not (ints and w < 2):
                    pe.wait_ge(picked_copied, b * PBANKS + (w - 1))
                for k in range(4):
                    pe.wait_ge(onehot_made, b * (4 * PBANKS) + (4 * w + k + 1))
                    for c in range(2):
                        for n in pair:
                            cols = slice((n % 2) * BLOCK, (n % 2 + 1) * BLOCK)
                            for part in range(PARTS):
                                first = k == 0 and c == 0 and part == 0
                                last = pe.matmul(p_pick[w % 2][:, cols], parts[:, n, part, 2 * k + c],
                                                 onehot[:, k, c, cols], start=first and n == pair[0],
                                                 stop=k == 3 and c == 1 and part == PARTS - 1,
                                                 skip_group_check=True)
                    if k < 3:
                        last.then_inc(onehot_used, 1)
                last.then_inc(onehot_used, 1)

            def layer1(b, p, u):
                pe.wait_ge(z_in[p], (u + 1) * (16 * Z_LOADS))
                for n in range(N1):
                    if n < 2:
                        pe.wait_ge(y_copied, b + 1)
                    else:
                        pe.wait_ge(hid1_ready, b * N1 + (n - 1))
                    for c in range(ZCHUNKS):
                        k = ZROWS + DROWS[c]
                        last = pe.matmul(p_mlp[n % 2][:, 0:BLOCK], w1_sb[0:k, c, n * P:(n + 1) * P],
                                         z[0:k, p, c], start=c == 0, stop=c == ZCHUNKS - 1)
                    last.then_inc(sum1_done, 1)

            def layer2(b):
                pe.wait_ge(hid1_ready, (b + 1) * N1)
                for m in range(N2):
                    for n in range(N1):
                        last = pe.matmul(p_mlp[m][:, 0:BLOCK], w2_sb[:, n, m * P:(m + 1) * P],
                                         hid1[:, n], start=n == 0, stop=n == N1 - 1)
                    last.then_inc(sum2_done, 1)

            def layer3(b):
                pe.wait_ge(hid2_ready, (b + 1) * N2)
                for s in range(HALVES):
                    for m in range(N2):
                        last = pe.matmul(p_mlp[0][:, s:s + 1], hid2[:, m, s * P:(s + 1) * P],
                                         w3_sb[:, m:m + 1], start=m == 0, stop=m == N2 - 1)
                last.then_inc(y_done, 1)

            def step(b, p, u):
                whole = isinstance(b, int)
                turn(b, p, u)
                grams(b, p)
                later = not (whole and b == 0)
                more = not (whole and b == BLOCKS - 1)
                before = u - 1 + p if not whole else (b - 1) // 2
                if later:
                    layer1(b - 1, 1 - p, before)
                if more:
                    pick(b + 1, 0, False)
                    pick(b + 1, 1, False)
                if later:
                    layer2(b - 1)
                if more:
                    pick(b + 1, 2, False)
                    pick(b + 1, 3, False)
                if later:
                    layer3(b - 1)

            pe.wait_ge(ident_made, 1)
            pe.wait_ge(gram_zeroed, 1)
            for w in range(PBANKS):
                pick(0, w, True)
            pe.wait_ge(weights_in, 16 * WEIGHT_LOADS)
            blocks(pe, step)
            layer1(BLOCKS - 1, 1, BLOCKS // 2 - 1)
            layer2(BLOCKS - 1)
            layer3(BLOCKS - 1)

        @block.scalar
        def _(act):
            def high(n):
                act.wait_ge(table_in[n % 2], 16 * (n // 2 + 1))
                act.activation(parts[:, n, 0].rearrange("p c d -> p (c d)"), stage[:, n % 2], ACT.Copy)\
                    .then_inc(part_high, 1)

            def mid(n):
                act.wait_ge(part_rest, n + 1)
                act.activation(parts[:, n, 1].rearrange("p c d -> p (c d)"), rest[:], ACT.Copy)\
                    .then_inc(part_mid, 1)

            for n in range(NP):
                high(n)
                mid(n)

            def layer1_out(b):
                for n in range(N1):
                    act.wait_ge(sum1_done, b * N1 + (n + 1))
                    act.activation(hid1[:, n], p_mlp[n % 2][:, 0:BLOCK], ACT.Relu, bias=b1_sb[:, n:n + 1])\
                        .then_inc(hid1_ready, 1)

            def layer2_out(b):
                for m in range(N2):
                    act.wait_ge(sum2_done, b * N2 + (m + 1))
                    act.activation(hid2[:, m], p_mlp[m][:, 0:BLOCK], ACT.Relu, bias=b2_sb[:, m:m + 1])\
                        .then_inc(hid2_ready, 1)

            def step(b, p, u):
                whole = isinstance(b, int)
                for h in range(HALVES):
                    for g in range(GROUPS):
                        r = h * GROUPS + g
                        act.wait_ge(turned, b * TBANKS + (r + 1))
                        act.activation(emb_t[:, p, g * GROUP:(g + 1) * GROUP, h * P:(h + 1) * P],
                                       p_turn[r % 2][:].rearrange("p (k s) -> p k s", k=GROUP), ACT.Copy)\
                            .then_inc(turned_copied, 1)
                for v in range(GBANKS):
                    h, from_ = v // (HSPAN // FILL), v % (HSPAN // FILL) * FILL
                    act.wait_ge(gram_done, b * GBANKS + (v + 1))
                    if v == 0 and not (whole and b == 0):
                        act.wait_ge(gram_stored, b * 32)
                    at = h * HSPAN + from_
                    act.activation(gram[:, :, at:at + FILL],
                                   p_gram[v % 2][:, 0:FILL * F].rearrange("p (k f) -> p f k", f=F), ACT.Copy)\
                        .then_inc(gram_copied, 1)
                if not (whole and b == 0):
                    layer1_out(b - 1)
                    layer2_out(b - 1)

            act.wait_ge(weights_in, 16 * WEIGHT_LOADS)
            blocks(act, step)
            layer1_out(BLOCKS - 1)
            layer2_out(BLOCKS - 1)

        @block.vector
        def _(dve):
            dve.memset(y_sb[:], 0.0).then_inc(y_copied, 1)
            dve.memset(p_gram[0][:], 0.0)
            dve.memset(p_gram[1][:], 0.0).then_inc(gram_zeroed, 1)
            dve.wait_ge(rows_counted, 1)
            dve.tensor_copy(row_no[:], row_int[:]).then_inc(rows_known, 1)
            dve.wait_ge(rows_known, 1)
            for n in range(NP):
                dve.wait_ge(part_high, n + 1)
                if n >= 1:
                    dve.wait_ge(table_split, n)
                dve.tensor_tensor(rest[:], stage[:, n % 2], parts[:, n, 0].rearrange("p c d -> p (c d)"),
                                  ALU.subtract).then_inc(part_rest, 1)
                dve.wait_ge(part_mid, n + 1)
                dve.tensor_tensor(parts[:, n, 2].rearrange("p c d -> p (c d)"), rest[:],
                                  parts[:, n, 1].rearrange("p c d -> p (c d)"),
                                  ALU.subtract).then_inc(table_split, 1)

            def narrow(b):
                dve.wait_ge(wide_in, (b + 1) * 16)
                dve.tensor_copy(ids_half[:], ids_wide[:]).then_inc(ids_halved, 1)
                dve.wait_ge(ids_halved, b + 1)

            def make(b, w):
                have = min(2, NP - 2 * w)
                for k in range(4):
                    if not (isinstance(b, int) and b == 0 and w == 0):
                        dve.wait_ge(onehot_used, b * (4 * PBANKS) + (4 * w + k - 3))
                    for c in range(2):
                        last = dve.tensor_scalar(
                            onehot[:, k, c, 0:have * BLOCK],
                            ids_half[:, 2 * w:2 * w + have].rearrange("p n s -> p (n s)"),
                            row_no[0:ROWS, 2 * k + c:2 * k + c + 1], None, ALU.is_equal)
                    last.then_inc(onehot_made, 1)

            def copy_picked(b, p, w):
                have = min(2, NP - 2 * w)
                dve.wait_ge(onehot_used, b * (4 * PBANKS) + 4 * (w + 1))
                dve.tensor_copy(emb_t[:, p, NG + 2 * w:NG + 2 * w + have].rearrange("p n s -> p (n s)"),
                                p_pick[w % 2][:, 0:have * BLOCK]).then_inc(picked_copied, 1)

            def look_up(b, p):
                narrow(b)
                for w in range(PBANKS):
                    make(b, w)
                    if w >= 1:
                        copy_picked(b, p, w - 1)
                copy_picked(b, p, PBANKS - 1)

            def copy_y(b):
                dve.wait_ge(y_done, b + 1)
                dve.tensor_copy(y_sb[:, bass.ds(b, 1)].rearrange("p o h -> p (o h)"),
                                p_mlp[0][:, 0:HALVES]).then_inc(y_copied, 1)

            def step(b, p, u):
                whole = isinstance(b, int)
                if not (whole and b == BLOCKS - 1):
                    look_up(b + 1, 1 - p)
                if not (whole and b == 0):
                    copy_y(b - 1)

            look_up(0, 0)
            blocks(dve, step)
            copy_y(BLOCKS - 1)


def kernel(**inputs):
    import numpy as _np
    import concourse.bacc as _bacc
    from concourse import mybir as _mybir
    from concourse.bass_utils import run_bass_kernel_spmd as _run

    nc = _bacc.Bacc("TRN2", target_bir_lowering=False, num_devices=1)
    given = {n: _np.asarray(a) for n, a in inputs.items()}
    ids = given["ids"]
    laid = {
        "ids_g": ids[:, GATHERED].reshape(BLOCKS, HALVES, P, NG).transpose(0, 2, 1, 3),
        "ids_p": ids[:, PICKED].reshape(BLOCKS, BLOCK, NP).transpose(0, 2, 1),
        "dense_t": given["dense_ctx"].reshape(BLOCKS, HALVES, QUADS, HSPAN, DENSE)
        .transpose(4, 0, 2, 1, 3).reshape(DENSE, BLOCKS, BLOCK),
        "w1_pairs": given["W_top1"][pair_rows()],
        "w1_dense": given["W_top1"][F * (F - 1) // 2:],
        "b1": given["b_top1"], "w2": given["W_top2"], "b2": given["b_top2"], "w3": given["W_top3"],
    }
    laid |= {f"tbl_{f}": given[f"tbl_{f}"] for f in range(F)}
    arrays, ap = {}, {}
    for name, a in laid.items():
        a = _np.ascontiguousarray(a)
        arrays[f"in_{name}"] = a
        ap[name] = nc.dram_tensor(f"in_{name}", a.shape, _mybir.dt.from_np(a.dtype), kind="ExternalInput").ap()
    out = nc.dram_tensor("out_y", (P, BLOCKS * HALVES), _mybir.dt.float32, kind="ExternalOutput").ap()
    dlrm_tower(nc, ap["ids_g"], ap["ids_p"], [ap[f"tbl_{f}"] for f in range(F)], ap["dense_t"],
               ap["w1_pairs"], ap["w1_dense"], ap["b1"], ap["w2"], ap["b2"], ap["w3"], out)
    y = _run(nc, [arrays], core_ids=[0]).results[0]["out_y"]
    y = y.reshape(QUADS // HALVES, HALVES, HSPAN, BLOCKS, HALVES).transpose(3, 1, 4, 0, 2)
    return _np.ascontiguousarray(y.reshape(SAMPLES, 1))
```

```python
import concourse.bass as bass
from concourse import mybir
from contextlib import ExitStack

VOCAB = [12500, 1250, 1250, 12500, 12500, 1250, 1250, 1000, 1000, 12500, 125000, 1250, 12500, 12500,
         12500, 12500, 1000, 1000, 1000, 1000, 1250, 1000, 1000, 1250, 1000, 1250, 1000]
F = len(VOCAB)
D = 128
SAMPLES = 2048
DENSE = 16
H1, H2 = 512, 256

P = 128
BLOCK = 256
BLOCKS = SAMPLES // BLOCK
HALVES = BLOCK // P
CHUNKS = 8
PICKED = [f for f in range(F) if VOCAB[f] == 1000][:9]
GATHERED = [f for f in range(F) if f not in PICKED]
ROWS = 1000 // CHUNKS
PLACES = GATHERED + PICKED
NG, NP = len(GATHERED), len(PICKED)
ROWS_T = F + NP
GROUP = 3
GROUPS = NG // GROUP
TBANKS = HALVES * GROUPS
PBANKS = (NP + 1) // 2
ONEHOTS = 4
QUADS = 4
SPAN = BLOCK // QUADS
HSPAN = P // QUADS
FILL = 16
GBANKS = BLOCK // (QUADS * FILL)
RING = (F - 1) // 2
WRAPPED = F + RING
ZCHUNKS = 3
AROWS = F // ZCHUNKS
ZROWS = AROWS * RING
DROWS = [0, 5, 11]
DFROM = [0, 0, 5]
N1, N2 = H1 // P, H2 // P


def pair_rows():
    rows = []
    for c in range(ZCHUNKS):
        for k in range(1, RING + 1):
            for a in range(c * AROWS, (c + 1) * AROWS):
                i, j = PLACES[a], PLACES[(a + k) % F]
                i, j = max(i, j), min(i, j)
                rows.append(i * (i - 1) // 2 + j)
    return rows


def row_of(place, p):
    return NP + place if p else F - 1 - place


def dlrm_tower(nc, ids_g, ids_p, tables, dense_t, w1_pairs, w1_dense, b1, w2, b2, w3, out):
    f32, f32r = mybir.dt.float32, mybir.dt.float32r
    i32, f16 = mybir.dt.int32, mybir.dt.float16
    ALU = mybir.AluOpType
    ACT = mybir.ActivationFunctionType

    ctx = ExitStack()
    with ctx:
        def sb(name, shape, dt):
            return ctx.enter_context(nc.sbuf_tensor(name, shape, dt))

        def pb(name):
            return ctx.enter_context(nc.psum_tensor(name, [P, 512], f32))

        def sem(name):
            return ctx.enter_context(nc.semaphore(name))

        idx = sb("idx", [P, 2, HALVES, NG], i32)
        emb = sb("emb", [P, 2, HALVES, NG, D], f32)
        emb_t = sb("emb_t", [P, ROWS_T, BLOCK], f32)
        parts = sb("parts", [ROWS, NP, 2, CHUNKS, D], f32r)
        ids_wide = sb("ids_wide", [ROWS, 2, 2 * BLOCK], i32)
        ids_half = sb("ids_half", [ROWS, 2, 2 * BLOCK], f16)
        row_int = sb("row_int", [P, CHUNKS], i32)
        row_no = sb("row_no", [P, CHUNKS], f32)
        onehot = sb("onehot", [ROWS, ONEHOTS, 2 * BLOCK], f32r)
        ident = sb("ident", [P, P], f32)
        gram = sb("gram", [P, F, SPAN], f32)
        z = sb("z", [P, ZCHUNKS, BLOCK], f32)
        z_parts = sb("z_parts", [P, 2, ZCHUNKS, BLOCK], f32r)
        w1_parts = sb("w1_parts", [P, 2, ZCHUNKS, H1], f32r)
        w2_parts = sb("w2_parts", [P, 2, N1, H2], f32r)
        w3_sb = sb("w3_sb", [P, N2], f32)
        b1_sb = sb("b1_sb", [P, N1], f32)
        b2_sb = sb("b2_sb", [P, N2], f32)
        hid = sb("hid", [P, 2, BLOCK], f32)
        hid1_parts = sb("hid1_parts", [P, 2, N1, BLOCK], f32r)
        y_sb = sb("y_sb", [P, BLOCKS, HALVES], f32)

        stage = emb_t[0:ROWS, NP:F].rearrange("p f s -> p (f s)")
        STAGES = (F - NP) * BLOCK // (CHUNKS * D)
        w1_stage = emb_t[:, F:ROWS_T].rearrange("p f s -> p (f s)")
        w2_stage = gram[:].rearrange("p f s -> p (f s)")

        gram_dram = nc.dram_tensor("gram_dram", (2, QUADS, 32, WRAPPED, SPAN), f32, kind="Internal").ap()

        p_turn = [pb(f"p_turn{i}") for i in range(2)]
        p_pick = [pb(f"p_pick{i}") for i in range(2)]
        p_gram = [pb(f"p_gram{i}") for i in range(2)]
        p_mlp = [pb(f"p_mlp{i}") for i in range(2)]

        table_in = [sem(f"table_in{i}") for i in range(STAGES)]
        weights_in = sem("weights_in")
        idx_in = [[sem(f"idx_in{p}{h}") for h in range(HALVES)] for p in range(2)]
        wide_in = [sem(f"wide_in{i}") for i in range(2)]
        gathers_begun = sem("gathers_begun")
        gathered = [[[sem(f"gathered{p}{h}{g}") for g in range(GROUPS)] for h in range(HALVES)]
                    for p in range(2)]
        z_in = [sem(f"z_in{c}") for c in range(ZCHUNKS)]
        z_in_last = sem("z_in_last")
        ident_zeroed = sem("ident_zeroed")
        ident_made = sem("ident_made")
        rows_counted = sem("rows_counted")
        rows_known = sem("rows_known")
        gram_zeroed = sem("gram_zeroed")
        table_high = sem("table_high")
        table_split = sem("table_split")
        weight_high = sem("weight_high")
        weight_split = sem("weight_split")
        ids_halved = sem("ids_halved")
        onehot_made = sem("onehot_made")
        onehot_used = sem("onehot_used")
        picked_copied = sem("picked_copied")
        turned = sem("turned")
        turned_copied = sem("turned_copied")
        odd_copied = sem("odd_copied")
        gram_done = sem("gram_done")
        gram_copied = sem("gram_copied")
        gram_stored = sem("gram_stored")
        z_high = sem("z_high")
        z_split = sem("z_split")
        sum1_done = sem("sum1_done")
        hid1_out = sem("hid1_out")
        hid1_high = sem("hid1_high")
        hid1_split = sem("hid1_split")
        sum2_done = sem("sum2_done")
        hid2_out = sem("hid2_out")
        y_done = sem("y_done")
        y_copied = sem("y_copied")
        y_stored = sem("y_stored")

        WEIGHT_LOADS = ZCHUNKS + 2 + 4
        WEIGHT_PIECES = ZCHUNKS + 1
        Z_LOADS = [QUADS + (d > 0) for d in DROWS]
        ZK = [ZROWS + d for d in DROWS]

        LAST = BLOCKS - 1
        turn_banks = p_turn + p_pick
        sum1_banks = p_mlp + p_pick

        def before(b, p, u):
            return b - 1, 1 - p, (u + p - 1)

        def after(b, p, u):
            return b + 1, 1 - p, (u + p)

        def embeddings(p, place, n, sample, samples):
            step = row_of(1, p) - row_of(0, p)
            return bass.AP(emb_t, row_of(place, p) * BLOCK + sample,
                           [[ROWS_T * BLOCK, P], [step * BLOCK, n]] + ([[1, samples]] if samples > 1 else []))

        def is_(b, n):
            return isinstance(b, int) and b == n

        def blocks(eng, step):
            step(0, 0, 0)
            with eng.Fori(0, BLOCKS // 2 - 1) as i:
                step(i * 2 + 1, 1, i)
                step(i * 2 + 2, 0, i + 1)
            step(BLOCKS - 1, 1, BLOCKS // 2 - 1)

        def tables_of(w):
            return range(2 * w, min(2 * w + 2, NP))

        GROUP_PAIRS = [range(g, g + 2) for g in range(0, GROUPS, 2)]

        def load_pairs(eng, p, c, loaded):
            for q in range(QUADS):
                a = c * AROWS
                at = a if p else F - 1 - a
                step = WRAPPED if p else -WRAPPED
                pairs = bass.AP(gram_dram.tensor, (((p * QUADS + q) * 32 + at) * WRAPPED + a + 1) * SPAN,
                                [[SPAN, RING], [(step + 1) * SPAN, AROWS], [1, SPAN]])
                eng.dma_start(z[0:ZROWS, c, q * SPAN:(q + 1) * SPAN], pairs).then_inc(loaded, 16)

        block = ctx.enter_context(nc.Block())

        @block.sync
        def _(sp):
            def load_idx(b, p, h):
                sp.dma_start(idx[:, p, h], ids_g[bass.ds(b, 1), h].rearrange("o p g -> (o p) g"))\
                    .then_inc(idx_in[p][h], 16)

            def load_wide(b, p, w):
                n = len(tables_of(w))
                sp.dma_start(ids_wide[:, (p + w) % 2, 0:n * BLOCK],
                             ids_p[bass.ds(b, 1), 2 * w:2 * w + n].rearrange("o n s -> o (n s)")
                             .broadcast_to([ROWS, n * BLOCK])).then_inc(wide_in[(p + w) % 2], 16)

            def load_table(n):
                if n >= STAGES:
                    sp.wait_ge(table_split, n - STAGES + 1)
                sp.dma_start(stage[:, n % STAGES * CHUNKS * D:(n % STAGES + 1) * CHUNKS * D],
                             tables[PICKED[n]].rearrange("(p c) d -> p (c d)", c=CHUNKS))\
                    .then_inc(table_in[n % STAGES], 16)

            load_idx(0, 0, 0)
            load_idx(0, 0, 1)
            load_idx(1, 1, 0)
            for w in range(PBANKS):
                if w >= 2:
                    sp.wait_ge(ids_halved, w - 1)
                load_wide(0, 0, w)
                for n in tables_of(w):
                    load_table(n)
            for c in range(ZCHUNKS):
                sp.dma_start(w1_stage[0:ZROWS, c * H1:(c + 1) * H1], w1_pairs[c * ZROWS:(c + 1) * ZROWS, :])\
                    .then_inc(weights_in, 16)
                if DROWS[c]:
                    sp.dma_start(w1_stage[ZROWS:ZK[c], c * H1:(c + 1) * H1],
                                 w1_dense[DFROM[c]:DFROM[c] + DROWS[c], :]).then_inc(weights_in, 16)
            sp.dma_start(w2_stage[:, 0:N1 * H2].rearrange("p (k n) -> p k n", k=N1),
                         w2.rearrange("(k p) n -> p k n", p=P)).then_inc(weights_in, 16)
            with nc.allow_non_contiguous_dma(reason="small vectors, one value per partition"):
                sp.dma_start(w3_sb[:], w3.rearrange("(k p) o -> p (k o)", p=P)).then_inc(weights_in, 16)
                sp.dma_start(b1_sb[:], b1.rearrange("(k p) -> p k", p=P)).then_inc(weights_in, 16)
                sp.dma_start(b2_sb[:], b2.rearrange("(k p) -> p k", p=P)).then_inc(weights_in, 16)
            for w in range(2):
                sp.wait_ge(ids_halved, PBANKS + w - 1)
                load_wide(1, 1, w)

            def load_z(b, p):
                sp.wait_ge(gram_stored, (b + 1) * 32)
                for c in range(ZCHUNKS):
                    load_pairs(sp, p, c, z_in[c])
                    if DROWS[c]:
                        load_dense(b, c)

            def load_dense(b, c):
                sp.dma_start(z[ZROWS:ZK[c], c],
                             dense_t[DFROM[c]:DFROM[c] + DROWS[c], bass.ds(b, 1), :]
                             .rearrange("d o s -> d (o s)")).then_inc(z_in[c], 16)

            def wide_ahead(b, p, w):
                sp.wait_ge(ids_halved, (b + 1) * PBANKS + (w - 1))
                if w < PBANKS:
                    load_wide(b + 1, 1 - p, w)
                else:
                    load_wide(b + 2, p, w - PBANKS)

            def step(b, p, u):
                more, has_old = not is_(b, BLOCKS - 1), not is_(b, 0)
                if more:
                    if has_old:
                        sp.wait_ge(turned, b * TBANKS)
                    load_idx(b + 1, 1 - p, 1)
                    wide_ahead(b, p, 2)
                    wide_ahead(b, p, 3)
                if has_old:
                    old, old_p, _ = before(b, p, u)
                    load_z(old, old_p)
                if more:
                    sp.wait_ge(turned, b * TBANKS + GROUPS)
                    load_idx(b + 2, p, 0)
                    for w in range(4, PBANKS + 2):
                        wide_ahead(b, p, w)
                sp.wait_ge(gram_copied, (b + 1) * GBANKS)
                rows = gram_dram[p].rearrange("q a b s -> (q a) b s")
                sp.dma_start(rows[:, 0:F], gram[:]).then_inc(gram_stored, 16)
                sp.dma_start(rows[:, F:WRAPPED], gram[:, 0:RING]).then_inc(gram_stored, 16)

            blocks(sp, step)
            sp.wait_ge(z_split, (BLOCKS - 1) * ZCHUNKS)
            for c in range(ZCHUNKS):
                if DROWS[c]:
                    load_dense(LAST, c)
            sp.wait_ge(gram_stored, BLOCKS * 32)
            for c in range(ZCHUNKS - 1):
                load_pairs(sp, 1, c, z_in[c])
            sp.wait_ge(idx_in[0][0], 16 * (BLOCKS // 2 + 1))
            for w in range(2):
                sp.wait_ge(wide_in[w], 16 * (BLOCKS * PBANKS // 2 + 1))
            sp.wait_ge(y_copied, BLOCKS + 1)
            sp.dma_start(out, y_sb[:].rearrange("p b h -> p (b h)")).then_inc(y_stored, 16)
            sp.wait_ge(y_stored, 16)

        @block.gpsimd
        def _(pool):
            pool.iota(row_int[:], pattern=[[1, CHUNKS]], base=0, channel_multiplier=CHUNKS)\
                .then_inc(rows_counted, 1)
            pool.memset(ident[:], 0.0).then_inc(ident_zeroed, 1)
            pool.wait_ge(ident_zeroed, 1)
            pool.affine_select(out=ident[:], in_=ident[:], compare_op=ALU.not_equal, fill=1.0, base=0,
                               pattern=[[-1, P]], channel_multiplier=1).then_inc(ident_made, 1)

            def step(b, p, u):
                for h in range(HALVES):
                    pool.wait_ge(idx_in[p][h], (u + 1) * 16)
                    pool.sem_inc(gathers_begun, 1)
                    for g in range(NG):
                        pool.indirect_dma_start(
                            emb[:, p, h, g], None, tables[GATHERED[g]],
                            bass.IndirectOffsetOnAxis(idx[:, p, h, g:g + 1], 0),
                        ).then_inc(gathered[p][h][g // GROUP], 16)

            blocks(pool, step)
            pool.wait_ge(z_split, LAST * ZCHUNKS)
            pool.wait_ge(gram_stored, BLOCKS * 32)
            load_pairs(pool, 1, ZCHUNKS - 1, z_in_last)

        @block.tensor
        def _(pe):
            def turn(b, p, u, h, groups):
                for g in groups:
                    r = h * GROUPS + g
                    pe.wait_ge(gathered[p][h][g], (u + 1) * (16 * GROUP))
                    if is_(b, LAST):
                        if r < 2:
                            pe.wait_ge(turned_copied, LAST * TBANKS + (r - 1))
                        elif r < 4:
                            pe.wait_ge(picked_copied, BLOCKS * PBANKS)
                        elif r % 2 == 0:
                            pe.wait_ge(turned_copied, LAST * TBANKS + (r - 4) // 2 + 1)
                        else:
                            pe.wait_ge(odd_copied, (r - 4) // 2 + 1)
                        bank = turn_banks[r % 4]
                    else:
                        if not (is_(b, 0) and r < 2):
                            pe.wait_ge(turned_copied, b * TBANKS + (r - 1))
                        bank = p_turn[r % 2]
                    for k in range(GROUP):
                        last = pe.transpose(bank[:, k * P:(k + 1) * P],
                                            emb[:, p, h, g * GROUP + k], ident[:])
                    last.then_inc(turned, 1)

            def grams(b, p, h):
                if is_(b, LAST):
                    pe.wait_ge(turned_copied, LAST * TBANKS + (h + 1) * GROUPS // 2)
                    pe.wait_ge(odd_copied, (h + 1) * GROUPS // 2)
                else:
                    pe.wait_ge(turned_copied, b * TBANKS + (h + 1) * GROUPS)
                if h == 0:
                    pe.wait_ge(picked_copied, (b + 1) * PBANKS)
                for part in range(HSPAN // FILL):
                    v = h * (HSPAN // FILL) + part
                    if not (is_(b, 0) and v < 2):
                        pe.wait_ge(gram_copied, b * GBANKS + (v - 1))
                    for k in range(FILL):
                        for q in range(QUADS):
                            s = h * P + q * HSPAN + part * FILL + k
                            e = emb_t[:, 0 if p == 0 else NP:F if p == 0 else ROWS_T, s]
                            last = pe.matmul(p_gram[v % 2][32 * q:32 * q + F, k * F:(k + 1) * F],
                                             e, e, start=True, stop=True)
                    last.then_inc(gram_done, 1)

            def pick(b, p, u, w):
                if is_(b, 0):
                    pe.wait_ge(table_split, tables_of(w)[-1] + 1)
                if not (is_(b, 0) and w < 2):
                    pe.wait_ge(picked_copied, b * PBANKS + (w - 1))
                for c in range(CHUNKS):
                    pe.wait_ge(onehot_made, b * (CHUNKS * PBANKS) + (CHUNKS * w + c + 1))
                    for n in tables_of(w):
                        cols = slice(n % 2 * BLOCK, (n % 2 + 1) * BLOCK)
                        for part in range(2):
                            last = pe.matmul(p_pick[(p + w) % 2][:, cols], parts[:, n, part, c],
                                             onehot[:, c % ONEHOTS, cols],
                                             start=c == 0 and part == 0 and n % 2 == 0,
                                             stop=c == CHUNKS - 1 and part == 1, skip_group_check=True)
                    last.then_inc(onehot_used, 1)

            def product1(bank, n, c):
                for wp, zp in ((0, 0), (0, 1), (1, 0)):
                    last = pe.matmul(bank[:, 0:BLOCK], w1_parts[0:ZK[c], wp, c, n * P:(n + 1) * P],
                                     z_parts[0:ZK[c], zp, c], start=c == 0 and wp == zp == 0,
                                     stop=c == ZCHUNKS - 1 and wp == 1)
                return last

            def layer1(b, p, u):
                pe.wait_ge(z_split, (b + 1) * ZCHUNKS)
                for n in range(N1):
                    if n == 0:
                        pe.wait_ge(y_copied, b + 1)
                    elif n >= 2:
                        pe.wait_ge(hid1_out, b * N1 + (n - 1))
                    for c in range(ZCHUNKS):
                        last = product1(p_mlp[n % 2], n, c)
                    last.then_inc(sum1_done, 1)

            def layer1_last():
                pe.wait_ge(y_copied, LAST + 1)
                for c in range(ZCHUNKS):
                    pe.wait_ge(z_split, LAST * ZCHUNKS + c + 1)
                    for n in range(N1):
                        last = product1(sum1_banks[n], n, c)
                        if c == ZCHUNKS - 1:
                            last.then_inc(sum1_done, 1)

            def product2(bank, m, n):
                for wp, hp in ((0, 0), (0, 1), (1, 0)):
                    last = pe.matmul(bank[:, 0:BLOCK], w2_parts[:, wp, n, m * P:(m + 1) * P],
                                     hid1_parts[:, hp, n], start=n == 0 and wp == hp == 0,
                                     stop=n == N1 - 1 and wp == 1)
                return last

            def layer2(b):
                pe.wait_ge(hid1_split, (b + 1) * N1)
                for m in range(N2):
                    for n in range(N1):
                        last = product2(p_mlp[m], m, n)
                    last.then_inc(sum2_done, 1)

            def layer2_last():
                for n in range(N1):
                    pe.wait_ge(hid1_split, LAST * N1 + n + 1)
                    for m in range(N2):
                        last = product2(p_turn[m], m, n)
                        if n == N1 - 1:
                            last.then_inc(sum2_done, 1)

            def layer3(b):
                pe.wait_ge(hid2_out, (b + 1) * N2)
                for s in range(HALVES):
                    for m in range(N2):
                        last = pe.matmul(p_mlp[0][:, s:s + 1], hid[:, m, s * P:(s + 1) * P],
                                         w3_sb[:, m:m + 1], start=m == 0, stop=m == N2 - 1)
                last.then_inc(y_done, 1)

            def step(b, p, u):
                nxt, old = after(b, p, u), before(b, p, u)
                if is_(b, BLOCKS - 1):
                    for h in range(HALVES):
                        turn(b, p, u, h, range(GROUPS))
                        grams(b, p, h)
                    layer1(*old)
                    layer2(old[0])
                    layer3(old[0])
                    return
                has_old = not is_(b, 0)
                for k in range(3):
                    turn(b, p, u, 0, GROUP_PAIRS[k])
                    pick(*nxt, k)
                grams(b, p, 0)
                turn(b, p, u, 1, GROUP_PAIRS[0])
                pick(*nxt, 3)
                if has_old:
                    layer1(*old)
                turn(b, p, u, 1, GROUP_PAIRS[1])
                pick(*nxt, 4)
                if has_old:
                    layer2(old[0])
                turn(b, p, u, 1, GROUP_PAIRS[2])
                if has_old:
                    layer3(old[0])
                grams(b, p, 1)

            pe.wait_ge(ident_made, 1)
            pe.wait_ge(gram_zeroed, 1)
            for w in range(PBANKS):
                pick(0, 0, 0, w)
            pe.wait_ge(weight_split, WEIGHT_PIECES)
            blocks(pe, step)
            layer1_last()
            layer2_last()
            layer3(LAST)

        @block.scalar
        def _(act):
            def halve_ids(b, p, u, w):
                cols = slice(0, len(tables_of(w)) * BLOCK)
                s = (p + w) % 2
                act.wait_ge(wide_in[s], u * (16 * PBANKS) + 16 * ((PBANKS * p + w) // 2 + 1))
                act.activation(ids_half[:, s, cols], ids_wide[:, s, cols], ACT.Copy).then_inc(ids_halved, 1)

            def copy_picked(b, p, w):
                n = tables_of(w)
                act.wait_ge(onehot_used, b * (CHUNKS * PBANKS) + CHUNKS * (w + 1))
                act.activation(embeddings(p, NG + n[0], len(n), 0, BLOCK),
                               p_pick[(p + w) % 2][:, 0:len(n) * BLOCK].rearrange("p (n s) -> p n s", s=BLOCK),
                               ACT.Copy).then_inc(picked_copied, 1)

            def copy_turned(b, p, h, groups):
                for g in groups:
                    r = h * GROUPS + g
                    if is_(b, LAST) and r % 2:
                        continue
                    act.wait_ge(turned, b * TBANKS + (r + 1))
                    bank = turn_banks[r % 4] if is_(b, LAST) else p_turn[r % 2]
                    act.activation(embeddings(p, g * GROUP, GROUP, h * P, P),
                                   bank[:, 0:GROUP * P].rearrange("p (k s) -> p k s", k=GROUP),
                                   ACT.Copy).then_inc(turned_copied, 1)

            def copy_gram(b, p, h):
                for part in range(HSPAN // FILL):
                    v = h * (HSPAN // FILL) + part
                    act.wait_ge(gram_done, b * GBANKS + (v + 1))
                    if v == 0 and not is_(b, 0):
                        act.wait_ge(gram_stored, b * 32)
                    columns = bass.AP(gram, (0 if p else F - 1) * SPAN + v * FILL,
                                      [[F * SPAN, P], [SPAN if p else -SPAN, F], [1, FILL]])
                    act.activation(columns, p_gram[v % 2][:, 0:FILL * F].rearrange("p (k f) -> p f k", f=F),
                                   ACT.Copy)\
                        .then_inc(gram_copied, 1)

            def high_of_z(b):
                if is_(b, BLOCKS - 1):
                    act.wait_ge(sum1_done, b * N1)
                for c in range(ZCHUNKS):
                    if is_(b, LAST) and c == ZCHUNKS - 1:
                        act.wait_ge(z_in[c], 16 * (BLOCKS * Z_LOADS[c] - QUADS))
                        act.wait_ge(z_in_last, 16 * QUADS)
                    else:
                        act.wait_ge(z_in[c], (b + 1) * (16 * Z_LOADS[c]))
                    act.activation(z_parts[0:ZK[c], 0, c], z[0:ZK[c], c], ACT.Copy).then_inc(z_high, 1)

            def layer1_out(b):
                for n in range(N1):
                    act.wait_ge(sum1_done, b * N1 + (n + 1))
                    if n >= 2:
                        act.wait_ge(hid1_split, b * N1 + (n - 1))
                    bank = sum1_banks[n] if is_(b, LAST) else p_mlp[n % 2]
                    act.activation(hid[:, n % 2], bank[:, 0:BLOCK], ACT.Relu, bias=b1_sb[:, n:n + 1])\
                        .then_inc(hid1_out, 1)
                    act.wait_ge(hid1_out, b * N1 + (n + 1))
                    act.activation(hid1_parts[:, 0, n], hid[:, n % 2], ACT.Copy).then_inc(hid1_high, 1)

            def layer2_out(b):
                for m in range(N2):
                    act.wait_ge(sum2_done, b * N2 + (m + 1))
                    bank = p_turn[m] if is_(b, LAST) else p_mlp[m]
                    act.activation(hid[:, m], bank[:, 0:BLOCK], ACT.Relu, bias=b2_sb[:, m:m + 1])\
                        .then_inc(hid2_out, 1)

            for w in range(PBANKS):
                for n in tables_of(w):
                    act.wait_ge(table_in[n % STAGES], 16 * (n // STAGES + 1))
                    act.activation(parts[:, n, 0].rearrange("p c d -> p (c d)"),
                                   stage[:, n % STAGES * CHUNKS * D:(n % STAGES + 1) * CHUNKS * D], ACT.Copy)\
                        .then_inc(table_high, 1)
                    if n == 2 * w:
                        if w >= 2:
                            copy_picked(0, 0, w - 2)
                        halve_ids(0, 0, 0, w)
            act.wait_ge(weights_in, 16 * WEIGHT_LOADS)
            for c in range(ZCHUNKS):
                act.activation(w1_parts[0:ZK[c], 0, c], w1_stage[0:ZK[c], c * H1:(c + 1) * H1], ACT.Copy)\
                    .then_inc(weight_high, 1)
            act.activation(w2_parts[:, 0].rearrange("p k n -> p (k n)"), w2_stage[:, 0:N1 * H2], ACT.Copy)\
                .then_inc(weight_high, 1)
            for w in range(PBANKS - 2, PBANKS):
                copy_picked(0, 0, w)
            halve_ids(1, 1, 0, 0)
            act.wait_ge(table_split, NP)
            act.wait_ge(weight_split, WEIGHT_PIECES)

            def step(b, p, u):
                nxt, old = after(b, p, u), before(b, p, u)
                if is_(b, BLOCKS - 1):
                    for h in range(HALVES):
                        copy_turned(b, p, h, range(GROUPS))
                        copy_gram(b, p, h)
                    high_of_z(old[0])
                    layer1_out(old[0])
                    layer2_out(old[0])
                    return
                has_old = not is_(b, 0)
                for k in range(3):
                    copy_turned(b, p, 0, GROUP_PAIRS[k])
                    if k == 0:
                        halve_ids(*nxt, 1)
                    copy_picked(nxt[0], nxt[1], k)
                    halve_ids(*nxt, k + 2)
                copy_gram(b, p, 0)
                copy_turned(b, p, 1, GROUP_PAIRS[0])
                if has_old:
                    high_of_z(old[0])
                copy_picked(nxt[0], nxt[1], 3)
                if has_old:
                    layer1_out(old[0])
                copy_turned(b, p, 1, GROUP_PAIRS[1])
                copy_picked(nxt[0], nxt[1], 4)
                halve_ids(b + 2, p, u + 1, 0)
                if has_old:
                    layer2_out(old[0])
                copy_turned(b, p, 1, GROUP_PAIRS[2])
                copy_gram(b, p, 1)

            blocks(act, step)
            high_of_z(BLOCKS - 1)
            layer1_out(BLOCKS - 1)
            layer2_out(BLOCKS - 1)

        @block.vector
        def _(dve):
            def make(b, p, w, chunks):
                cols = slice(0, len(tables_of(w)) * BLOCK)
                if chunks[0] == 0:
                    dve.wait_ge(ids_halved, b * PBANKS + (w + 1))
                for c in chunks:
                    if not (is_(b, 0) and w == 0 and c < ONEHOTS):
                        dve.wait_ge(onehot_used, b * (CHUNKS * PBANKS) + (CHUNKS * w + c - ONEHOTS + 1))
                    dve.tensor_scalar(onehot[:, c % ONEHOTS, cols], ids_half[:, (p + w) % 2, cols],
                                      row_no[0:ROWS, c:c + 1], None, ALU.is_equal).then_inc(onehot_made, 1)

            early, late = range(0, ONEHOTS), range(ONEHOTS, CHUNKS)

            def copy_odd():
                for r in range(1, TBANKS, 2):
                    h, g = r // GROUPS, r % GROUPS
                    dve.wait_ge(turned, LAST * TBANKS + r + 1)
                    dve.tensor_copy(embeddings(1, g * GROUP, GROUP, h * P, P),
                                    turn_banks[r % 4][:, 0:GROUP * P].rearrange("p (k s) -> p k s", k=GROUP))\
                        .then_inc(odd_copied, 1)

            def low_of_z(b):
                for c in range(ZCHUNKS):
                    dve.wait_ge(z_high, b * ZCHUNKS + (c + 1))
                    dve.tensor_tensor(z_parts[0:ZK[c], 1, c], z[0:ZK[c], c],
                                      z_parts[0:ZK[c], 0, c].bitcast(f32), ALU.subtract).then_inc(z_split, 1)

            def low_of_hid1(b):
                for n in range(N1):
                    dve.wait_ge(hid1_high, b * N1 + (n + 1))
                    dve.tensor_tensor(hid1_parts[:, 1, n], hid[:, n % 2], hid1_parts[:, 0, n].bitcast(f32),
                                      ALU.subtract).then_inc(hid1_split, 1)

            def copy_y(b):
                dve.wait_ge(y_done, b + 1)
                dve.tensor_copy(y_sb[:, bass.ds(b, 1)].rearrange("p o h -> p (o h)"),
                                p_mlp[0][:, 0:HALVES]).then_inc(y_copied, 1)

            dve.memset(y_sb[:], 0.0).then_inc(y_copied, 1)
            dve.memset(p_gram[0][:], 0.0)
            dve.memset(p_gram[1][:], 0.0).then_inc(gram_zeroed, 1)
            dve.wait_ge(rows_counted, 1)
            dve.tensor_copy(row_no[:], row_int[:]).then_inc(rows_known, 1)
            dve.wait_ge(rows_known, 1)
            for w in range(PBANKS):
                for n in tables_of(w):
                    dve.wait_ge(table_high, n + 1)
                    dve.tensor_tensor(parts[:, n, 1].rearrange("p c d -> p (c d)"),
                                      stage[:, n % STAGES * CHUNKS * D:(n % STAGES + 1) * CHUNKS * D],
                                      parts[:, n, 0].rearrange("p c d -> p (c d)").bitcast(f32),
                                      ALU.subtract).then_inc(table_split, 1)
                make(0, 0, w, range(CHUNKS))
            dve.wait_ge(weight_high, WEIGHT_PIECES)
            for c in range(ZCHUNKS):
                dve.tensor_tensor(w1_parts[0:ZK[c], 1, c], w1_stage[0:ZK[c], c * H1:(c + 1) * H1],
                                  w1_parts[0:ZK[c], 0, c].bitcast(f32), ALU.subtract).then_inc(weight_split, 1)
            dve.tensor_tensor(w2_parts[:, 1].rearrange("p k n -> p (k n)"), w2_stage[:, 0:N1 * H2],
                              w2_parts[:, 0].rearrange("p k n -> p (k n)").bitcast(f32),
                              ALU.subtract).then_inc(weight_split, 1)

            def step(b, p, u):
                nxt, nxt_p, _ = after(b, p, u)
                old, _, _ = before(b, p, u)
                more, has_old = not is_(b, BLOCKS - 1), not is_(b, 0)
                if more:
                    for w in range(3):
                        make(nxt, nxt_p, w, range(CHUNKS))
                    make(nxt, nxt_p, 3, range(CHUNKS))
                else:
                    copy_odd()
                if has_old:
                    low_of_z(old)
                if more:
                    make(nxt, nxt_p, 4, early)
                if has_old:
                    low_of_hid1(old)
                if more:
                    make(nxt, nxt_p, 4, late)
                if has_old:
                    copy_y(old)

            blocks(dve, step)
            low_of_z(BLOCKS - 1)
            low_of_hid1(BLOCKS - 1)
            copy_y(BLOCKS - 1)


def kernel(**inputs):
    import numpy as _np
    import concourse.bacc as _bacc
    from concourse import mybir as _mybir
    from concourse.bass_utils import run_bass_kernel_spmd as _run

    nc = _bacc.Bacc("TRN2", target_bir_lowering=False, num_devices=1)
    given = {n: _np.asarray(a) for n, a in inputs.items()}
    padded = _np.concatenate([given["ids"], _np.zeros((BLOCK, F), given["ids"].dtype)])
    laid = {
        "ids_g": padded[:, GATHERED].reshape(BLOCKS + 1, HALVES, P, NG),
        "ids_p": padded[:, PICKED].reshape(BLOCKS + 1, BLOCK, NP).transpose(0, 2, 1),
        "dense_t": given["dense_ctx"].reshape(BLOCKS, HALVES, QUADS, HSPAN, DENSE)
        .transpose(4, 0, 2, 1, 3).reshape(DENSE, BLOCKS, BLOCK),
        "w1_pairs": given["W_top1"][pair_rows()],
        "w1_dense": given["W_top1"][F * (F - 1) // 2:],
        "b1": given["b_top1"], "w2": given["W_top2"], "b2": given["b_top2"], "w3": given["W_top3"],
    }
    laid |= {f"tbl_{f}": given[f"tbl_{f}"] for f in range(F)}
    arrays, ap = {}, {}
    for name, a in laid.items():
        a = _np.ascontiguousarray(a)
        arrays[f"in_{name}"] = a
        ap[name] = nc.dram_tensor(f"in_{name}", a.shape, _mybir.dt.from_np(a.dtype), kind="ExternalInput").ap()
    out = nc.dram_tensor("out_y", (P, BLOCKS * HALVES), _mybir.dt.float32, kind="ExternalOutput").ap()
    dlrm_tower(nc, ap["ids_g"], ap["ids_p"], [ap[f"tbl_{f}"] for f in range(F)], ap["dense_t"],
               ap["w1_pairs"], ap["w1_dense"], ap["b1"], ap["w2"], ap["b2"], ap["w3"], out)
    y = _run(nc, [arrays], core_ids=[0]).results[0]["out_y"]
    y = y.reshape(QUADS // HALVES, HALVES, HSPAN, BLOCKS, HALVES).transpose(3, 1, 4, 0, 2)
    return _np.ascontiguousarray(y.reshape(SAMPLES, 1))
```

```python
import concourse.bass as bass
from concourse import mybir
from contextlib import ExitStack

VOCAB = [12500, 1250, 1250, 12500, 12500, 1250, 1250, 1000, 1000, 12500, 125000, 1250, 12500, 12500,
         12500, 12500, 1000, 1000, 1000, 1000, 1250, 1000, 1000, 1250, 1000, 1250, 1000]
F = len(VOCAB)
D = 128
SAMPLES = 2048
DENSE = 16
H1, H2 = 512, 256

P = 128
BLOCK = 256
BLOCKS = SAMPLES // BLOCK
HALVES = BLOCK // P
CHUNKS = 8
PICKED = [f for f in range(F) if VOCAB[f] == 1000][:10]
GATHERED = [f for f in range(F) if f not in PICKED] + PICKED[:1]
ROWS = 1000 // CHUNKS
PLACES = GATHERED + PICKED[1:]
NG, NP = len(GATHERED), len(PICKED)
ROWS_T = F + NP
GROUP = 3
GROUPS = NG // GROUP
TBANKS = HALVES * GROUPS
PBANKS = NP // 2
ONEHOTS = 4
QUADS = 4
SPAN = BLOCK // QUADS
HSPAN = P // QUADS
FILL = 16
GBANKS = BLOCK // (QUADS * FILL)
RING = (F - 1) // 2
WRAPPED = F + RING
ZCHUNKS = 3
AROWS = F // ZCHUNKS
ZROWS = AROWS * RING
DROWS = [0, 5, 11]
DFROM = [0, 0, 5]
N1, N2 = H1 // P, H2 // P


def pair_rows():
    rows = []
    for c in range(ZCHUNKS):
        for k in range(1, RING + 1):
            for a in range(c * AROWS, (c + 1) * AROWS):
                i, j = PLACES[a], PLACES[(a + k) % F]
                i, j = max(i, j), min(i, j)
                rows.append(i * (i - 1) // 2 + j)
    return rows


def row_of(place, p):
    return NP + place if p else F - 1 - place


def dlrm_tower(nc, ids_g, ids_p, tables, dense_t, w1_pairs, w1_dense, b1, w2, b2, w3, out):
    f32, f32r = mybir.dt.float32, mybir.dt.float32r
    i32, f16 = mybir.dt.int32, mybir.dt.float16
    ALU = mybir.AluOpType
    ACT = mybir.ActivationFunctionType

    ctx = ExitStack()
    with ctx:
        def sb(name, shape, dt):
            return ctx.enter_context(nc.sbuf_tensor(name, shape, dt))

        def pb(name):
            return ctx.enter_context(nc.psum_tensor(name, [P, 512], f32))

        def sem(name):
            return ctx.enter_context(nc.semaphore(name))

        idx = sb("idx", [P, HALVES, NG], i32)
        emb = sb("emb", [P, HALVES, NG, D], f32)
        emb_t = sb("emb_t", [P, ROWS_T, BLOCK], f32)
        parts = sb("parts", [ROWS, NP, 2, CHUNKS, D], f32r)
        ids_wide = sb("ids_wide", [ROWS, 2, 2 * BLOCK], i32)
        ids_half = sb("ids_half", [ROWS, 2, 2 * BLOCK], f16)
        row_int = sb("row_int", [P, CHUNKS], i32)
        row_no = sb("row_no", [P, CHUNKS], f32)
        onehot = sb("onehot", [ROWS, ONEHOTS, 2 * BLOCK], f32r)
        ident = sb("ident", [P, P], f32)
        gram = sb("gram", [P, F, SPAN], f32)
        z = sb("z", [P, ZCHUNKS, BLOCK], f32)
        z_parts = sb("z_parts", [P, 2, ZCHUNKS, BLOCK], f32r)
        w1_parts = sb("w1_parts", [P, 2, ZCHUNKS, H1], f32r)
        w2_parts = sb("w2_parts", [P, 2, N1, H2], f32r)
        w3_sb = sb("w3_sb", [P, N2], f32)
        b1_sb = sb("b1_sb", [P, N1], f32)
        b2_sb = sb("b2_sb", [P, N2], f32)
        hid = sb("hid", [P, 2, BLOCK], f32)
        hid1_parts = sb("hid1_parts", [P, 2, N1, BLOCK], f32r)
        y_sb = sb("y_sb", [P, BLOCKS, HALVES], f32)

        stage = emb_t[0:ROWS, F - NG:F].rearrange("p f s -> p (f s)")
        STAGES = NG * BLOCK // (CHUNKS * D)
        ODD_ROWS = CHUNKS * D // BLOCK
        odd_stage = emb_t[0:ROWS, F:F + ODD_ROWS].rearrange("p f s -> p (f s)")
        w1_stage = emb_t[:, F + ODD_ROWS:ROWS_T].rearrange("p f s -> p (f s)")
        w2_stage = gram[:].rearrange("p f s -> p (f s)")

        gram_dram = nc.dram_tensor("gram_dram", (2, QUADS, 32, WRAPPED, SPAN), f32, kind="Internal").ap()

        p_turn = [pb(f"p_turn{i}") for i in range(2)]
        p_pick = [pb(f"p_pick{i}") for i in range(2)]
        p_gram = [pb(f"p_gram{i}") for i in range(2)]
        p_mlp = [pb(f"p_mlp{i}") for i in range(2)]

        table_in = [sem(f"table_in{i}") for i in range(STAGES)]
        odd_in = sem("odd_in")
        w2_in = sem("w2_in")
        weights_in = sem("weights_in")
        idx_in = [sem(f"idx_in{h}") for h in range(HALVES)]
        wide_in = [sem(f"wide_in{i}") for i in range(2)]
        gathers_begun = sem("gathers_begun")
        gathered = [[[sem(f"gathered{p}{h}{g}") for g in range(GROUPS)] for h in range(HALVES)]
                    for p in range(2)]
        z_in = [sem(f"z_in{c}") for c in range(ZCHUNKS)]
        z_in_last = sem("z_in_last")
        ident_zeroed = sem("ident_zeroed")
        ident_made = sem("ident_made")
        rows_counted = sem("rows_counted")
        rows_known = sem("rows_known")
        gram_zeroed = sem("gram_zeroed")
        table_high = sem("table_high")
        table_split = sem("table_split")
        weight_high = sem("weight_high")
        weight_split = sem("weight_split")
        ids_halved = sem("ids_halved")
        onehot_made = sem("onehot_made")
        onehot_used = sem("onehot_used")
        picked_copied = sem("picked_copied")
        turned = sem("turned")
        turned_copied = sem("turned_copied")
        odd_copied = sem("odd_copied")
        gram_done = sem("gram_done")
        gram_copied = sem("gram_copied")
        gram_stored = sem("gram_stored")
        wrap_stored = sem("wrap_stored")
        z_high = sem("z_high")
        z_split = sem("z_split")
        sum1_done = sem("sum1_done")
        hid1_out = sem("hid1_out")
        hid1_high = sem("hid1_high")
        hid1_split = sem("hid1_split")
        sum2_done = sem("sum2_done")
        hid2_out = sem("hid2_out")
        y_done = sem("y_done")
        y_copied = sem("y_copied")
        y_stored = sem("y_stored")

        WEIGHT_LOADS = ZCHUNKS + 2 + 3
        WEIGHT_PIECES = 2 + ZCHUNKS
        Z_LOADS = [QUADS + (d > 0) for d in DROWS]
        ZK = [ZROWS + d for d in DROWS]

        LAST = BLOCKS - 1
        AHEAD = 3
        turn_banks = p_turn + p_pick
        sum1_banks = p_pick + p_gram

        def before(b, p, u):
            return b - 1, 1 - p, (u + p - 1)

        def after(b, p, u):
            return b + 1, 1 - p, (u + p)

        def embeddings(p, place, n, sample, samples):
            step = row_of(1, p) - row_of(0, p)
            return bass.AP(emb_t, row_of(place, p) * BLOCK + sample,
                           [[ROWS_T * BLOCK, P], [step * BLOCK, n]] + ([[1, samples]] if samples > 1 else []))

        def is_(b, n):
            return isinstance(b, int) and b == n

        def blocks(eng, step):
            step(0, 0, 0)
            with eng.Fori(0, BLOCKS // 2 - 1) as i:
                step(i * 2 + 1, 1, i)
                step(i * 2 + 2, 0, i + 1)
            step(LAST, 1, BLOCKS // 2 - 1)

        early, late = range(0, ONEHOTS), range(ONEHOTS, CHUNKS)

        def tables_of(w, p):
            return range(max(2 * w, 1 - p), 2 * w + 2)

        def columns(w, p):
            n = tables_of(w, p)
            return slice(n[0] % 2 * BLOCK, (n[-1] % 2 + 1) * BLOCK)

        def group(g, p):
            return range(g * GROUP, min((g + 1) * GROUP, NG - p))

        GROUP_PAIRS = [range(g, g + 2) for g in range(0, GROUPS, 2)]

        def load_pairs(eng, p, c, loaded):
            for q in range(QUADS):
                a = c * AROWS
                at = a if p else F - 1 - a
                step = WRAPPED if p else -WRAPPED
                pairs = bass.AP(gram_dram.tensor, (((p * QUADS + q) * 32 + at) * WRAPPED + a + 1) * SPAN,
                                [[SPAN, RING], [(step + 1) * SPAN, AROWS], [1, SPAN]])
                eng.dma_start(z[0:ZROWS, c, q * SPAN:(q + 1) * SPAN], pairs).then_inc(loaded, 16)

        def table_stage(n):
            at = (NP - 1 - n) % STAGES * CHUNKS * D
            return stage[:, at:at + CHUNKS * D]

        block = ctx.enter_context(nc.Block())

        @block.sync
        def _(sp):
            def load_idx(b, h):
                sp.dma_start(idx[:, h], ids_g[bass.ds(b, 1), h].rearrange("o p g -> (o p) g"))\
                    .then_inc(idx_in[h], 16)

            def load_wide(b, p, w):
                n, cols = tables_of(w, p), columns(w, p)
                sp.dma_start(ids_wide[:, (p + w) % 2, cols],
                             ids_p[bass.ds(b, 1), n[0]:n[-1] + 1].rearrange("o n s -> o (n s)")
                             .broadcast_to([ROWS, cols.stop - cols.start])).then_inc(wide_in[(p + w) % 2], 16)

            def load_table(n):
                if n > STAGES:
                    sp.wait_ge(table_split, n - STAGES)
                sp.dma_start(table_stage(n), tables[PICKED[n]].rearrange("(p c) d -> p (c d)", c=CHUNKS))\
                    .then_inc(table_in[(n - 1) % STAGES], 16)

            load_idx(0, 0)
            load_idx(0, 1)
            for w in range(PBANKS):
                if w >= 2:
                    sp.wait_ge(ids_halved, w - 1)
                load_wide(0, 0, w)
                for n in tables_of(w, 0):
                    load_table(n)
            sp.dma_start(odd_stage, tables[PICKED[0]].rearrange("(p c) d -> p (c d)", c=CHUNKS))\
                .then_inc(odd_in, 16)
            sp.dma_start(w2_stage[:, 0:N1 * H2].rearrange("p (k n) -> p k n", k=N1),
                         w2.rearrange("(k p) n -> p k n", p=P)).then_inc(w2_in, 16)
            for c in range(ZCHUNKS):
                sp.dma_start(w1_stage[0:ZROWS, c * H1:(c + 1) * H1], w1_pairs[c * ZROWS:(c + 1) * ZROWS, :])\
                    .then_inc(weights_in, 16)
                if DROWS[c]:
                    sp.dma_start(w1_stage[ZROWS:ZK[c], c * H1:(c + 1) * H1],
                                 w1_dense[DFROM[c]:DFROM[c] + DROWS[c], :]).then_inc(weights_in, 16)
            with nc.allow_non_contiguous_dma(reason="small vectors, one value per partition"):
                sp.dma_start(w3_sb[:], w3.rearrange("(k p) o -> p (k o)", p=P)).then_inc(weights_in, 16)
                sp.dma_start(b1_sb[:], b1.rearrange("(k p) -> p k", p=P)).then_inc(weights_in, 16)
                sp.dma_start(b2_sb[:], b2.rearrange("(k p) -> p k", p=P)).then_inc(weights_in, 16)
            for w in range(2):
                sp.wait_ge(ids_halved, PBANKS + w - 1)
                load_wide(1, 1, w)

            def load_z(b, p):
                sp.wait_ge(gram_stored, (b + 1) * 16)
                for c in range(ZCHUNKS):
                    if c == 1:
                        sp.wait_ge(wrap_stored, (b + 1) * 16)
                    load_pairs(sp, p, c, z_in[c])
                    if DROWS[c]:
                        load_dense(b, c)

            def load_dense(b, c):
                sp.dma_start(z[ZROWS:ZK[c], c],
                             dense_t[DFROM[c]:DFROM[c] + DROWS[c], bass.ds(b, 1), :]
                             .rearrange("d o s -> d (o s)")).then_inc(z_in[c], 16)

            def wide_ahead(b, p, w):
                sp.wait_ge(ids_halved, (b + 1) * PBANKS + (w - 1))
                if w < PBANKS:
                    load_wide(b + 1, 1 - p, w)
                else:
                    load_wide(b + 2, p, w - PBANKS)

            def step(b, p, u):
                more, has_old = not is_(b, LAST), not is_(b, 0)
                if more:
                    wide_ahead(b, p, 2)
                if has_old:
                    old, old_p, _ = before(b, p, u)
                    load_z(old, old_p)
                if more:
                    wide_ahead(b, p, 3)
                    for h in range(HALVES):
                        sp.wait_ge(turned, b * TBANKS + (h + 1) * GROUPS)
                        load_idx(b + 1, h)
                        for w in ((4, 5), (6,))[h]:
                            wide_ahead(b, p, w)
                sp.wait_ge(gram_copied, (b + 1) * GBANKS)
                rows = gram_dram[p].rearrange("q a b s -> (q a) b s")
                sp.dma_start(rows[:, 0:F], gram[:]).then_inc(gram_stored, 16)
                sp.dma_start(rows[:, F:WRAPPED], gram[:, 0:RING]).then_inc(wrap_stored, 16)

            blocks(sp, step)
            sp.wait_ge(z_split, LAST * ZCHUNKS)
            for c in range(ZCHUNKS):
                if DROWS[c]:
                    load_dense(LAST, c)
            sp.wait_ge(gram_stored, BLOCKS * 16)
            for c in range(ZCHUNKS - 1):
                if c == 1:
                    sp.wait_ge(wrap_stored, BLOCKS * 16)
                load_pairs(sp, 1, c, z_in[c])
            for w in range(2):
                sp.wait_ge(wide_in[w], 16 * (BLOCKS * PBANKS // 2 + 1))
            sp.wait_ge(y_copied, BLOCKS + 1)
            sp.dma_start(out, y_sb[:].rearrange("p b h -> p (b h)")).then_inc(y_stored, 16)
            sp.wait_ge(y_stored, 16)

        @block.gpsimd
        def _(pool):
            pool.iota(row_int[:], pattern=[[1, CHUNKS]], base=0, channel_multiplier=CHUNKS)\
                .then_inc(rows_counted, 1)
            pool.memset(ident[:], 0.0).then_inc(ident_zeroed, 1)
            pool.wait_ge(ident_zeroed, 1)
            pool.affine_select(out=ident[:], in_=ident[:], compare_op=ALU.not_equal, fill=1.0, base=0,
                               pattern=[[-1, P]], channel_multiplier=1).then_inc(ident_made, 1)

            def step(b, p, u):
                for h in range(HALVES):
                    pool.wait_ge(idx_in[h], (b + 1) * 16)
                    pool.sem_inc(gathers_begun, 1)
                    for g in range(NG - p):
                        pool.indirect_dma_start(
                            emb[:, h, g], None, tables[GATHERED[g]],
                            bass.IndirectOffsetOnAxis(idx[:, h, g:g + 1], 0),
                        ).then_inc(gathered[p][h][g // GROUP], 16)

            blocks(pool, step)
            pool.wait_ge(z_split, LAST * ZCHUNKS)
            pool.wait_ge(gram_stored, BLOCKS * 16)
            pool.wait_ge(wrap_stored, BLOCKS * 16)
            load_pairs(pool, 1, ZCHUNKS - 1, z_in_last)

        @block.tensor
        def _(pe):
            def turn(b, p, u, h, groups):
                for g in groups:
                    r = h * GROUPS + g
                    pe.wait_ge(gathered[p][h][g], (u + 1) * (16 * len(group(g, p))))
                    if is_(b, LAST) and h == 1:
                        if g < 2:
                            pe.wait_ge(turned_copied, LAST * TBANKS + (r - 1))
                        elif g < 4:
                            pe.wait_ge(picked_copied, BLOCKS * PBANKS)
                        elif g % 2 == 0:
                            pe.wait_ge(turned_copied, LAST * TBANKS + GROUPS + (g - 4) // 2 + 1)
                        else:
                            pe.wait_ge(odd_copied, (g - 4) // 2 + 1)
                        bank = turn_banks[g % 4]
                    else:
                        if not (is_(b, 0) and r < 2):
                            pe.wait_ge(turned_copied, b * TBANKS + (r - 1))
                        bank = p_turn[r % 2]
                    for k, place in enumerate(group(g, p)):
                        last = pe.transpose(bank[:, k * P:(k + 1) * P], emb[:, h, place], ident[:])
                    last.then_inc(turned, 1)

            def grams(b, p, h, quarters):
                if is_(b, LAST) and h == 1:
                    pe.wait_ge(turned_copied, LAST * TBANKS + GROUPS + GROUPS // 2)
                    pe.wait_ge(odd_copied, GROUPS // 2)
                else:
                    pe.wait_ge(turned_copied, b * TBANKS + (h + 1) * GROUPS)
                if h == 0:
                    pe.wait_ge(picked_copied, (b + 1) * PBANKS)
                for part in quarters:
                    v = h * (HSPAN // FILL) + part
                    if not (is_(b, 0) and v < 2):
                        pe.wait_ge(gram_copied, b * GBANKS + (v - 1))
                    for k in range(FILL):
                        for q in range(QUADS):
                            s = h * P + q * HSPAN + part * FILL + k
                            e = emb_t[:, 0 if p == 0 else NP:F if p == 0 else ROWS_T, s]
                            last = pe.matmul(p_gram[v % 2][32 * q:32 * q + F, k * F:(k + 1) * F],
                                             e, e, start=True, stop=True)
                    last.then_inc(gram_done, 1)

            def pick(b, p, u, w, chunks=range(CHUNKS)):
                if is_(b, 0):
                    pe.wait_ge(table_split, tables_of(w, p)[-1])
                if chunks[0] == 0 and not (is_(b, 0) and w < 2):
                    pe.wait_ge(picked_copied, b * PBANKS + (w - 1))
                for c in chunks:
                    pe.wait_ge(onehot_made, b * (CHUNKS * PBANKS) + (CHUNKS * w + c + 1))
                    for n in tables_of(w, p):
                        cols = slice(n % 2 * BLOCK, (n % 2 + 1) * BLOCK)
                        for part in range(2):
                            last = pe.matmul(p_pick[(p + w) % 2][:, cols], parts[:, n, part, c],
                                             onehot[:, c % ONEHOTS, cols],
                                             start=c == 0 and part == 0 and n == tables_of(w, p)[0],
                                             stop=c == CHUNKS - 1 and part == 1, skip_group_check=True)
                    last.then_inc(onehot_used, 1)

            def product1(bank, n, c):
                for wp, zp in ((0, 0), (0, 1), (1, 0)):
                    last = pe.matmul(bank[:, 0:BLOCK], w1_parts[0:ZK[c], wp, c, n * P:(n + 1) * P],
                                     z_parts[0:ZK[c], zp, c], start=c == 0 and wp == zp == 0,
                                     stop=c == ZCHUNKS - 1 and wp == 1)
                return last

            def layer1(b, p, u):
                pe.wait_ge(z_split, (b + 1) * ZCHUNKS)
                for n in range(N1):
                    if n == 0:
                        pe.wait_ge(y_copied, b + 1)
                    elif n >= 2:
                        pe.wait_ge(hid1_out, b * N1 + (n - 1))
                    for c in range(ZCHUNKS):
                        last = product1(p_mlp[n % 2], n, c)
                    last.then_inc(sum1_done, 1)

            def layer1_last(c):
                pe.wait_ge(z_split, LAST * ZCHUNKS + c + 1)
                if c == 0:
                    pe.wait_ge(gram_copied, BLOCKS * GBANKS)
                for n in range(N1):
                    last = product1(sum1_banks[n], n, c)
                    if c == ZCHUNKS - 1:
                        last.then_inc(sum1_done, 1)

            def product2(bank, m, n):
                for wp, hp in ((0, 0), (0, 1), (1, 0)):
                    last = pe.matmul(bank[:, 0:BLOCK], w2_parts[:, wp, n, m * P:(m + 1) * P],
                                     hid1_parts[:, hp, n], start=n == 0 and wp == hp == 0,
                                     stop=n == N1 - 1 and wp == 1)
                return last

            def layer2(b):
                pe.wait_ge(hid1_split, (b + 1) * N1)
                for m in range(N2):
                    for n in range(N1):
                        last = product2(p_mlp[m], m, n)
                    last.then_inc(sum2_done, 1)

            def layer2_last():
                for n in range(N1):
                    pe.wait_ge(hid1_split, LAST * N1 + n + 1)
                    for m in range(N2):
                        last = product2(p_turn[m], m, n)
                        if n == N1 - 1:
                            last.then_inc(sum2_done, 1)

            def layer3(b):
                pe.wait_ge(hid2_out, (b + 1) * N2)
                for s in range(HALVES):
                    for m in range(N2):
                        last = pe.matmul(p_mlp[0][:, s:s + 1], hid[:, m, s * P:(s + 1) * P],
                                         w3_sb[:, m:m + 1], start=m == 0, stop=m == N2 - 1)
                last.then_inc(y_done, 1)

            def step(b, p, u):
                nxt, old = after(b, p, u), before(b, p, u)
                turn(b, p, u, 0, GROUP_PAIRS[0])
                pick(b, p, u, 3, early)
                turn(b, p, u, 0, GROUP_PAIRS[1])
                pick(b, p, u, 3, late)
                turn(b, p, u, 0, GROUP_PAIRS[2])
                pick(b, p, u, 4)
                if is_(b, LAST):
                    grams(b, p, 0, range(2))
                    turn(b, p, u, 1, GROUP_PAIRS[0])
                    layer1(*old)
                    turn(b, p, u, 1, GROUP_PAIRS[1])
                    turn(b, p, u, 1, GROUP_PAIRS[2])
                    grams(b, p, 1, range(2))
                    pe.wait_ge(gram_stored, BLOCKS * 16)
                    layer2(old[0])
                    layer3(old[0])
                    return
                has_old = not is_(b, 0)
                if has_old:
                    pick(*nxt, 0, early)
                grams(b, p, 0, range(2))
                turn(b, p, u, 1, GROUP_PAIRS[0])
                if has_old:
                    pick(*nxt, 0, late)
                else:
                    pe.wait_ge(weight_split, 1)
                    pick(*nxt, 0)
                turn(b, p, u, 1, GROUP_PAIRS[1])
                pick(*nxt, 1)
                if has_old:
                    layer1(*old)
                turn(b, p, u, 1, GROUP_PAIRS[2])
                pick(*nxt, 2)
                if has_old:
                    grams(b, p, 1, range(1))
                    layer2(old[0])
                    grams(b, p, 1, range(1, 2))
                    layer3(old[0])
                else:
                    grams(b, p, 1, range(2))
                    pe.wait_ge(weight_split, WEIGHT_PIECES)

            pe.wait_ge(ident_made, 1)
            pe.wait_ge(gram_zeroed, 1)
            for w in range(AHEAD):
                pick(0, 0, 0, w)
            blocks(pe, step)
            for c in range(ZCHUNKS):
                layer1_last(c)
            layer2_last()
            pe.wait_ge(y_copied, LAST + 1)
            layer3(LAST)

        @block.scalar
        def _(act):
            def halve_ids(b, p, u, w):
                cols, s = columns(w, p), (p + w) % 2
                act.wait_ge(wide_in[s], u * (16 * PBANKS) + 16 * ((PBANKS * p + w) // 2 + 1))
                act.activation(ids_half[:, s, cols], ids_wide[:, s, cols], ACT.Copy).then_inc(ids_halved, 1)

            def copy_picked(b, p, w):
                n = tables_of(w, p)
                act.wait_ge(onehot_used, b * (CHUNKS * PBANKS) + CHUNKS * (w + 1))
                act.activation(embeddings(p, NG - 1 + n[0], len(n), 0, BLOCK),
                               p_pick[(p + w) % 2][:, columns(w, p)].rearrange("p (n s) -> p n s", s=BLOCK),
                               ACT.Copy).then_inc(picked_copied, 1)

            def copy_turned(b, p, h, groups):
                for g in groups:
                    r = h * GROUPS + g
                    shared = is_(b, LAST) and h == 1
                    if shared and g % 2:
                        continue
                    act.wait_ge(turned, b * TBANKS + (r + 1))
                    bank = turn_banks[g % 4] if shared else p_turn[r % 2]
                    n = len(group(g, p))
                    act.activation(embeddings(p, g * GROUP, n, h * P, P),
                                   bank[:, 0:n * P].rearrange("p (k s) -> p k s", k=n),
                                   ACT.Copy).then_inc(turned_copied, 1)

            def copy_gram(b, p, h, quarters=range(2)):
                for part in quarters:
                    v = h * (HSPAN // FILL) + part
                    act.wait_ge(gram_done, b * GBANKS + (v + 1))
                    if v == 0 and not is_(b, 0):
                        act.wait_ge(gram_stored, b * 16)
                        act.wait_ge(wrap_stored, b * 16)
                    by_place = bass.AP(gram, (0 if p else F - 1) * SPAN + v * FILL,
                                       [[F * SPAN, P], [SPAN if p else -SPAN, F], [1, FILL]])
                    act.activation(by_place, p_gram[v % 2][:, 0:FILL * F].rearrange("p (k f) -> p f k", f=F),
                                   ACT.Copy).then_inc(gram_copied, 1)

            def high_of_z(b):
                if is_(b, LAST):
                    act.wait_ge(sum1_done, b * N1)
                for c in range(ZCHUNKS):
                    if is_(b, LAST) and c == ZCHUNKS - 1:
                        act.wait_ge(z_in[c], 16 * (BLOCKS * Z_LOADS[c] - QUADS))
                        act.wait_ge(z_in_last, 16 * QUADS)
                    else:
                        act.wait_ge(z_in[c], (b + 1) * (16 * Z_LOADS[c]))
                    act.activation(z_parts[0:ZK[c], 0, c], z[0:ZK[c], c], ACT.Copy).then_inc(z_high, 1)

            def layer1_out(b):
                for n in range(N1):
                    act.wait_ge(sum1_done, b * N1 + (n + 1))
                    if n >= 2:
                        act.wait_ge(hid1_split, b * N1 + (n - 1))
                    bank = sum1_banks[n] if is_(b, LAST) else p_mlp[n % 2]
                    act.activation(hid[:, n % 2], bank[:, 0:BLOCK], ACT.Relu, bias=b1_sb[:, n:n + 1])\
                        .then_inc(hid1_out, 1)
                    act.wait_ge(hid1_out, b * N1 + (n + 1))
                    act.activation(hid1_parts[:, 0, n], hid[:, n % 2], ACT.Copy).then_inc(hid1_high, 1)

            def layer2_out(b):
                for m in range(N2):
                    act.wait_ge(sum2_done, b * N2 + (m + 1))
                    bank = p_turn[m] if is_(b, LAST) else p_mlp[m]
                    act.activation(hid[:, m], bank[:, 0:BLOCK], ACT.Relu, bias=b2_sb[:, m:m + 1])\
                        .then_inc(hid2_out, 1)

            def high_of_odd_and_w2():
                act.wait_ge(odd_in, 16)
                act.activation(parts[:, 0, 0].rearrange("p c d -> p (c d)"), odd_stage, ACT.Copy)\
                    .then_inc(weight_high, 1)
                act.wait_ge(w2_in, 16)
                act.activation(w2_parts[:, 0].rearrange("p k n -> p (k n)"), w2_stage[:, 0:N1 * H2], ACT.Copy)\
                    .then_inc(weight_high, 1)

            def high_of_w1():
                act.wait_ge(weights_in, 16 * WEIGHT_LOADS)
                for c in range(ZCHUNKS):
                    act.activation(w1_parts[0:ZK[c], 0, c], w1_stage[0:ZK[c], c * H1:(c + 1) * H1], ACT.Copy)\
                        .then_inc(weight_high, 1)

            def finish_pick(b, p, u, w):
                copy_picked(b, p, w)
                if w + 2 < PBANKS:
                    halve_ids(b, p, u, w + 2)
                elif not is_(b, LAST):
                    halve_ids(*after(b, p, u), w + 2 - PBANKS)

            for w in range(PBANKS):
                if w < 2:
                    halve_ids(0, 0, 0, w)
                for n in tables_of(w, 0):
                    act.wait_ge(table_in[(n - 1) % STAGES], 16 * ((n - 1) // STAGES + 1))
                    act.activation(parts[:, n, 0].rearrange("p c d -> p (c d)"), table_stage(n), ACT.Copy)\
                        .then_inc(table_high, 1)
                    if w >= 2 and n == 2 * w:
                        finish_pick(0, 0, 0, w - 2)

            def step(b, p, u):
                nxt, old = after(b, p, u), before(b, p, u)
                has_old = not is_(b, 0)
                for k in range(3):
                    if not has_old:
                        act.wait_ge(table_split, (NP - 4, NP - 2, NP - 1)[k])
                    copy_turned(b, p, 0, GROUP_PAIRS[k])
                    if k == 1:
                        finish_pick(b, p, u, 3)
                finish_pick(b, p, u, 4)
                if is_(b, LAST):
                    copy_gram(b, p, 0)
                    copy_turned(b, p, 1, GROUP_PAIRS[0])
                    high_of_z(old[0])
                    layer1_out(old[0])
                    copy_turned(b, p, 1, GROUP_PAIRS[1])
                    copy_turned(b, p, 1, GROUP_PAIRS[2])
                    copy_gram(b, p, 1)
                    layer2_out(old[0])
                    return
                if not has_old:
                    high_of_odd_and_w2()
                    act.wait_ge(weight_split, 2)
                copy_gram(b, p, 0)
                copy_turned(b, p, 1, GROUP_PAIRS[0])
                finish_pick(*nxt, 0)
                copy_turned(b, p, 1, GROUP_PAIRS[1])
                if has_old:
                    high_of_z(old[0])
                else:
                    high_of_w1()
                finish_pick(*nxt, 1)
                if has_old:
                    layer1_out(old[0])
                copy_turned(b, p, 1, GROUP_PAIRS[2])
                if not has_old:
                    act.wait_ge(weight_split, WEIGHT_PIECES)
                finish_pick(*nxt, 2)
                copy_gram(b, p, 1, range(1))
                if has_old:
                    layer2_out(old[0])
                copy_gram(b, p, 1, range(1, 2))

            blocks(act, step)
            high_of_z(LAST)
            layer1_out(LAST)
            layer2_out(LAST)

        @block.vector
        def _(dve):
            def make(b, p, w, chunks):
                cols = columns(w, p)
                if chunks[0] == 0:
                    dve.wait_ge(ids_halved, b * PBANKS + (w + 1))
                for c in chunks:
                    if not (is_(b, 0) and w == 0 and c < ONEHOTS):
                        dve.wait_ge(onehot_used, b * (CHUNKS * PBANKS) + (CHUNKS * w + c - ONEHOTS + 1))
                    dve.tensor_scalar(onehot[:, c % ONEHOTS, cols], ids_half[:, (p + w) % 2, cols],
                                      row_no[0:ROWS, c:c + 1], None, ALU.is_equal).then_inc(onehot_made, 1)

            def copy_odd(groups):
                for g in groups:
                    if g % 2:
                        dve.wait_ge(turned, LAST * TBANKS + GROUPS + g + 1)
                        n = len(group(g, 1))
                        dve.tensor_copy(embeddings(1, g * GROUP, n, P, P),
                                        turn_banks[g % 4][:, 0:n * P].rearrange("p (k s) -> p k s", k=n))\
                            .then_inc(odd_copied, 1)

            def low_of_z(b):
                for c in range(ZCHUNKS):
                    dve.wait_ge(z_high, b * ZCHUNKS + (c + 1))
                    dve.tensor_tensor(z_parts[0:ZK[c], 1, c], z[0:ZK[c], c],
                                      z_parts[0:ZK[c], 0, c].bitcast(f32), ALU.subtract).then_inc(z_split, 1)

            def low_of_hid1(b):
                for n in range(N1):
                    dve.wait_ge(hid1_high, b * N1 + (n + 1))
                    dve.tensor_tensor(hid1_parts[:, 1, n], hid[:, n % 2], hid1_parts[:, 0, n].bitcast(f32),
                                      ALU.subtract).then_inc(hid1_split, 1)

            def copy_y(b):
                dve.wait_ge(y_done, b + 1)
                dve.tensor_copy(y_sb[:, bass.ds(b, 1)].rearrange("p o h -> p (o h)"),
                                p_mlp[0][:, 0:HALVES]).then_inc(y_copied, 1)

            dve.memset(y_sb[:], 0.0).then_inc(y_copied, 1)
            dve.memset(p_gram[0][:], 0.0)
            dve.memset(p_gram[1][:], 0.0).then_inc(gram_zeroed, 1)
            dve.wait_ge(rows_counted, 1)
            dve.tensor_copy(row_no[:], row_int[:]).then_inc(rows_known, 1)
            dve.wait_ge(rows_known, 1)

            def low_of_table(n):
                dve.wait_ge(table_high, n)
                dve.tensor_tensor(parts[:, n, 1].rearrange("p c d -> p (c d)"), table_stage(n),
                                  parts[:, n, 0].rearrange("p c d -> p (c d)").bitcast(f32),
                                  ALU.subtract).then_inc(table_split, 1)

            make(0, 0, 0, early)
            low_of_table(1)
            make(0, 0, 0, late)
            for w in range(1, AHEAD):
                for n in tables_of(w, 0):
                    low_of_table(n)
                make(0, 0, w, range(CHUNKS))
            for n in tables_of(AHEAD, 0):
                low_of_table(n)
            make(0, 0, AHEAD, early)

            def low_of_odd_and_w2():
                dve.wait_ge(weight_high, 1)
                dve.tensor_tensor(parts[:, 0, 1].rearrange("p c d -> p (c d)"), odd_stage,
                                  parts[:, 0, 0].rearrange("p c d -> p (c d)").bitcast(f32), ALU.subtract)\
                    .then_inc(weight_split, 1)
                dve.wait_ge(weight_high, 2)
                dve.tensor_tensor(w2_parts[:, 1].rearrange("p k n -> p (k n)"), w2_stage[:, 0:N1 * H2],
                                  w2_parts[:, 0].rearrange("p k n -> p (k n)").bitcast(f32),
                                  ALU.subtract).then_inc(weight_split, 1)

            def low_of_w1():
                for c in range(ZCHUNKS):
                    dve.wait_ge(weight_high, 3 + c)
                    dve.tensor_tensor(w1_parts[0:ZK[c], 1, c], w1_stage[0:ZK[c], c * H1:(c + 1) * H1],
                                      w1_parts[0:ZK[c], 0, c].bitcast(f32), ALU.subtract)\
                        .then_inc(weight_split, 1)

            def step(b, p, u):
                nxt, nxt_p, _ = after(b, p, u)
                old, _, _ = before(b, p, u)
                has_old = not is_(b, 0)
                if not has_old:
                    low_of_table(NP - 2)
                make(b, p, 3, late)
                if not has_old:
                    low_of_table(NP - 1)
                make(b, p, 4, range(CHUNKS))
                if is_(b, LAST):
                    copy_odd(GROUP_PAIRS[0])
                    low_of_z(old)
                    low_of_hid1(old)
                    copy_odd(GROUP_PAIRS[1])
                    copy_odd(GROUP_PAIRS[2])
                    return
                make(nxt, nxt_p, 0, early)
                if not has_old:
                    low_of_odd_and_w2()
                make(nxt, nxt_p, 0, late)
                make(nxt, nxt_p, 1, range(CHUNKS))
                if not has_old:
                    low_of_w1()
                if has_old:
                    low_of_z(old)
                make(nxt, nxt_p, 2, early)
                if has_old:
                    low_of_hid1(old)
                make(nxt, nxt_p, 2, late)
                make(nxt, nxt_p, 3, early)
                if has_old:
                    copy_y(old)

            blocks(dve, step)
            low_of_z(LAST)
            copy_y(LAST - 1)
            low_of_hid1(LAST)
            copy_y(LAST)


def kernel(**inputs):
    import numpy as _np
    import concourse.bacc as _bacc
    from concourse import mybir as _mybir
    from concourse.bass_utils import run_bass_kernel_spmd as _run

    nc = _bacc.Bacc("TRN2", target_bir_lowering=False, num_devices=1)
    given = {n: _np.asarray(a) for n, a in inputs.items()}
    padded = _np.concatenate([given["ids"], _np.zeros((BLOCK, F), given["ids"].dtype)])
    laid = {
        "ids_g": given["ids"][:, GATHERED].reshape(BLOCKS, HALVES, P, NG),
        "ids_p": padded[:, PICKED].reshape(BLOCKS + 1, BLOCK, NP).transpose(0, 2, 1),
        "dense_t": given["dense_ctx"].reshape(BLOCKS, HALVES, QUADS, HSPAN, DENSE)
        .transpose(4, 0, 2, 1, 3).reshape(DENSE, BLOCKS, BLOCK),
        "w1_pairs": given["W_top1"][pair_rows()],
        "w1_dense": given["W_top1"][F * (F - 1) // 2:],
        "b1": given["b_top1"], "w2": given["W_top2"], "b2": given["b_top2"], "w3": given["W_top3"],
    }
    laid |= {f"tbl_{f}": given[f"tbl_{f}"] for f in range(F)}
    arrays, ap = {}, {}
    for name, a in laid.items():
        a = _np.ascontiguousarray(a)
        arrays[f"in_{name}"] = a
        ap[name] = nc.dram_tensor(f"in_{name}", a.shape, _mybir.dt.from_np(a.dtype), kind="ExternalInput").ap()
    out = nc.dram_tensor("out_y", (P, BLOCKS * HALVES), _mybir.dt.float32, kind="ExternalOutput").ap()
    dlrm_tower(nc, ap["ids_g"], ap["ids_p"], [ap[f"tbl_{f}"] for f in range(F)], ap["dense_t"],
               ap["w1_pairs"], ap["w1_dense"], ap["b1"], ap["w2"], ap["b2"], ap["w3"], out)
    y = _run(nc, [arrays], core_ids=[0]).results[0]["out_y"]
    y = y.reshape(QUADS // HALVES, HALVES, HSPAN, BLOCKS, HALVES).transpose(3, 1, 4, 0, 2)
    return _np.ascontiguousarray(y.reshape(SAMPLES, 1))
```
